# Optimizing a Trainium2 kernel written in Bass

```python
import numpy as np
import jax
import jax.numpy as jnp

def _softmax(x, axis=-1):
    return jax.nn.softmax(x, axis=axis)

def _gelu(x):
    return jax.nn.gelu(x, approximate=True)

def _silu(x):
    return jax.nn.silu(x)

def _sigmoid(x):
    return jax.nn.sigmoid(x)

def _layernorm(x, axis=-1, eps=1e-05):
    m = jnp.mean(x, axis=axis, keepdims=True)
    v = jnp.var(x, axis=axis, keepdims=True)
    return (x - m) / jnp.sqrt(v + eps)

def _scatter_add(tgt, idx, src, axis=0):
    return tgt.at[idx].add(src)

def _segment_sum(src, seg, n):
    return jax.ops.segment_sum(src, seg, n)
kernel_name = 'mk_gnn_ffn_d1_gnn_r8_b8a4d5'

def setup_inputs(seed: int=0):
    np.random.seed(seed)
    _w = jnp.asarray

    def _rec_inputs():
        import jax
        import jax.numpy as jnp
        _gk = jax.random.key(seed)
        x = -0.0001126 + 1 * jax.random.normal(jax.random.fold_in(_gk, 1), (1250, 768), jnp.float32)
        _s = jax.random.randint(jax.random.fold_in(_gk, 2), (20000,), 0, 1250, jnp.int32)
        _d = jax.random.randint(jax.random.fold_in(_gk, 3), (20000,), 0, 1250, jnp.int32)
        _loop = jnp.arange(1250, dtype=jnp.int32)
        src = jnp.concatenate([_s, _d, _loop])
        dst = jnp.concatenate([_d, _s, _loop])
        _o = jnp.argsort(dst, stable=True)
        src = src[_o]
        dst = dst[_o]
        return (x, src, dst)
    x, src, dst = _rec_inputs()

    def _L0_gnn_setup():
        import jax, jax.numpy as jnp
        import numpy as np
        NEG_SLOPE = 0.2

        def _gat_layer(x, W, a_src, a_dst, b, src, dst, n_nodes):
            h = x @ W
            e_src = h @ a_src
            e_dst = h @ a_dst
            e = jax.nn.leaky_relu(e_src[src] + e_dst[dst], NEG_SLOPE)
            m = jax.ops.segment_max(e, dst, num_segments=n_nodes)
            w = jnp.exp(e - m[dst])
            z = jax.ops.segment_sum(w, dst, num_segments=n_nodes)
            alpha = w / z[dst]
            out = jax.ops.segment_sum(h[src] * alpha[:, None], dst, num_segments=n_nodes)
            return out + b
        key = jax.random.key(seed)
        ks = jax.random.split(key, 10)
        N, E, D = (1250, 12500, 768)
        scale = 1.0 / np.sqrt(D)
        x = jax.random.normal(ks[0], (N, D), dtype=jnp.float32)
        edge_index = jax.random.randint(ks[1], (2, E), 0, N, dtype=jnp.int32)
        params = {}
        for i, nm in enumerate(['1', '2']):
            params[f'W{nm}'] = jax.random.normal(ks[2 + 4 * i], (D, D), jnp.float32) * scale
            params[f'att_src{nm}'] = jax.random.normal(ks[3 + 4 * i], (D,), jnp.float32) * scale
            params[f'att_dst{nm}'] = jax.random.normal(ks[4 + 4 * i], (D,), jnp.float32) * scale
            params[f'b{nm}'] = jnp.zeros((D,), jnp.float32)
        return {'x': x, 'edge_index': edge_index, **params}
    _L0_gnn_all = _L0_gnn_setup()
    _L0_gnn_in = {k: v for k, v in _L0_gnn_all.items() if k in ('W1', 'att_src1', 'att_dst1', 'b1', 'W2', 'att_src2', 'att_dst2', 'b2')}
    del _L0_gnn_all

    def _L0_ffn_setup():
        import jax, jax.numpy as jnp
        import numpy as np
        DIM = 768
        FF = 384
        E = 8
        K = 2
        H = 12
        HD = DIM // H
        LN_EPS = 1e-05

        def _layernorm(x, g, b):
            m = jnp.mean(x, axis=-1, keepdims=True)
            v = jnp.var(x, axis=-1, keepdims=True)
            return (x - m) * jax.lax.rsqrt(v + LN_EPS) * g + b

        def _attention(x, Wqkv, Wproj):
            B, T, D = x.shape
            qkv = (x @ Wqkv).reshape(B, T, 3, H, HD)
            q, k, v = (qkv[:, :, 0], qkv[:, :, 1], qkv[:, :, 2])
            scores = jnp.einsum('bqhd,bkhd->bhqk', q, k) * jnp.float32(HD) ** (-0.5)
            attn = jax.nn.softmax(scores, axis=-1)
            out = jnp.einsum('bhqk,bkhd->bqhd', attn, v).reshape(B, T, D)
            return out @ Wproj

        def _moe(x, Wrouter, W1, W2):
            B, T, D = x.shape
            xf = x.reshape(-1, D)
            N = xf.shape[0]
            logits = xf @ Wrouter
            topk_w, topk_idx = jax.lax.top_k(logits, K)
            topk_w = jax.nn.softmax(topk_w.astype(jnp.float32), axis=-1).astype(x.dtype)
            we = jnp.zeros((N, E), x.dtype).at[jnp.arange(N)[:, None], topk_idx].add(topk_w)

            def body(acc, expert):
                W1e, W2e, we_e = expert
                h = jax.nn.gelu(xf @ W1e, approximate=False)
                return (acc + we_e[:, None] * (h @ W2e), None)
            out, _ = jax.lax.scan(body, jnp.zeros_like(xf), (W1, W2, we.T))
            return out.reshape(B, T, D)
        key = jax.random.key(seed)
        ks = jax.random.split(key, 7)
        B, T = (4, 1024)
        init = lambda k, shape, fan: jax.random.normal(k, shape, jnp.float32) * fan ** (-0.5)
        return {'x': jax.random.normal(ks[0], (B, T, DIM), jnp.float32), 'Wqkv': init(ks[1], (DIM, 3 * DIM), DIM), 'Wproj': init(ks[2], (DIM, DIM), DIM), 'Wrouter': init(ks[3], (DIM, E), DIM), 'W1': init(ks[4], (E, DIM, FF), DIM), 'W2': init(ks[5], (E, FF, DIM), FF), 'ln1_g': jnp.ones((DIM,), jnp.float32), 'ln1_b': jnp.zeros((DIM,), jnp.float32), 'ln2_g': jnp.ones((DIM,), jnp.float32), 'ln2_b': jnp.zeros((DIM,), jnp.float32)}
    _L0_ffn_all = _L0_ffn_setup()
    _L0_ffn_in = {k: v for k, v in _L0_ffn_all.items() if k in ('Wqkv', 'Wproj', 'Wrouter', 'W1', 'W2', 'ln1_g', 'ln1_b', 'ln2_g', 'ln2_b')}
    del _L0_ffn_all
    return {'x': x, 'src': src, 'dst': dst, 'L0_gnn_W1': _L0_gnn_in['W1'], 'L0_gnn_att_src1': _L0_gnn_in['att_src1'], 'L0_gnn_att_dst1': _L0_gnn_in['att_dst1'], 'L0_gnn_b1': _L0_gnn_in['b1'], 'L0_gnn_W2': _L0_gnn_in['W2'], 'L0_gnn_att_src2': _L0_gnn_in['att_src2'], 'L0_gnn_att_dst2': _L0_gnn_in['att_dst2'], 'L0_gnn_b2': _L0_gnn_in['b2'], 'L0_ffn_Wqkv': _L0_ffn_in['Wqkv'], 'L0_ffn_Wproj': _L0_ffn_in['Wproj'], 'L0_ffn_Wrouter': _L0_ffn_in['Wrouter'], 'L0_ffn_W1': _L0_ffn_in['W1'], 'L0_ffn_W2': _L0_ffn_in['W2'], 'L0_ffn_ln1_g': _L0_ffn_in['ln1_g'], 'L0_ffn_ln1_b': _L0_ffn_in['ln1_b'], 'L0_ffn_ln2_g': _L0_ffn_in['ln2_g'], 'L0_ffn_ln2_b': _L0_ffn_in['ln2_b']}

def reference(x, src, dst, L0_gnn_W1, L0_gnn_att_src1, L0_gnn_att_dst1, L0_gnn_b1, L0_gnn_W2, L0_gnn_att_src2, L0_gnn_att_dst2, L0_gnn_b2, L0_ffn_Wqkv, L0_ffn_Wproj, L0_ffn_Wrouter, L0_ffn_W1, L0_ffn_W2, L0_ffn_ln1_g, L0_ffn_ln1_b, L0_ffn_ln2_g, L0_ffn_ln2_b):
    import jax
    import jax.numpy as jnp

    def _L0_gnn_ref(x, edge_index, W1, att_src1, att_dst1, b1, W2, att_src2, att_dst2, b2):
        import jax, jax.numpy as jnp
        import numpy as np
        NEG_SLOPE = 0.2

        def _gat_layer(x, W, a_src, a_dst, b, src, dst, n_nodes):
            h = x @ W
            e_src = h @ a_src
            e_dst = h @ a_dst
            e = jax.nn.leaky_relu(e_src[src] + e_dst[dst], NEG_SLOPE)
            m = jax.ops.segment_max(e, dst, num_segments=n_nodes)
            w = jnp.exp(e - m[dst])
            z = jax.ops.segment_sum(w, dst, num_segments=n_nodes)
            alpha = w / z[dst]
            out = jax.ops.segment_sum(h[src] * alpha[:, None], dst, num_segments=n_nodes)
            return out + b
        n_nodes = x.shape[0]
        loops = jnp.arange(n_nodes, dtype=edge_index.dtype)
        src = jnp.concatenate([edge_index[0], loops])
        dst = jnp.concatenate([edge_index[1], loops])
        h = _gat_layer(x, W1, att_src1, att_dst1, b1, src, dst, n_nodes)
        h = jax.nn.relu(h)
        out = _gat_layer(h, W2, att_src2, att_dst2, b2, src, dst, n_nodes)
        return out

    def _L0_ffn_ref(x, Wqkv, Wproj, Wrouter, W1, W2, ln1_g, ln1_b, ln2_g, ln2_b):
        import jax, jax.numpy as jnp
        import numpy as np
        DIM = 768
        FF = 384
        E = 8
        K = 2
        H = 12
        HD = DIM // H
        LN_EPS = 1e-05

        def _layernorm(x, g, b):
            m = jnp.mean(x, axis=-1, keepdims=True)
            v = jnp.var(x, axis=-1, keepdims=True)
            return (x - m) * jax.lax.rsqrt(v + LN_EPS) * g + b

        def _attention(x, Wqkv, Wproj):
            B, T, D = x.shape
            qkv = (x @ Wqkv).reshape(B, T, 3, H, HD)
            q, k, v = (qkv[:, :, 0], qkv[:, :, 1], qkv[:, :, 2])
            scores = jnp.einsum('bqhd,bkhd->bhqk', q, k) * jnp.float32(HD) ** (-0.5)
            attn = jax.nn.softmax(scores, axis=-1)
            out = jnp.einsum('bhqk,bkhd->bqhd', attn, v).reshape(B, T, D)
            return out @ Wproj

        def _moe(x, Wrouter, W1, W2):
            B, T, D = x.shape
            xf = x.reshape(-1, D)
            N = xf.shape[0]
            logits = xf @ Wrouter
            topk_w, topk_idx = jax.lax.top_k(logits, K)
            topk_w = jax.nn.softmax(topk_w.astype(jnp.float32), axis=-1).astype(x.dtype)
            we = jnp.zeros((N, E), x.dtype).at[jnp.arange(N)[:, None], topk_idx].add(topk_w)

            def body(acc, expert):
                W1e, W2e, we_e = expert
                h = jax.nn.gelu(xf @ W1e, approximate=False)
                return (acc + we_e[:, None] * (h @ W2e), None)
            out, _ = jax.lax.scan(body, jnp.zeros_like(xf), (W1, W2, we.T))
            return out.reshape(B, T, D)
        x = x + _attention(_layernorm(x, ln1_g, ln1_b), Wqkv, Wproj)
        x = x + _moe(_layernorm(x, ln2_g, ln2_b), Wrouter, W1, W2)
        return x
    edge_index = jnp.stack([src, dst])
    x = x + _L0_gnn_ref(_layernorm(x, axis=-1), edge_index, L0_gnn_W1, L0_gnn_att_src1, L0_gnn_att_dst1, L0_gnn_b1, L0_gnn_W2, L0_gnn_att_src2, L0_gnn_att_dst2, L0_gnn_b2)
    x = x + _L0_ffn_ref(_layernorm(x, axis=-1)[None], L0_ffn_Wqkv, L0_ffn_Wproj, L0_ffn_Wrouter, L0_ffn_W1, L0_ffn_W2, L0_ffn_ln1_g, L0_ffn_ln1_b, L0_ffn_ln2_g, L0_ffn_ln2_b)[0]
    return x

_drawn_inputs = setup_inputs


def setup_inputs(seed=0):
    import zlib

    import numpy as np

    out = dict(_drawn_inputs(seed))
    spreads = {'L0_gnn_b1': (0.0, 0.1),
     'L0_gnn_b2': (0.0, 0.1),
     'L0_ffn_ln1_g': (1.0, 0.2),
     'L0_ffn_ln1_b': (0.0, 0.1),
     'L0_ffn_ln2_g': (1.0, 0.2),
     'L0_ffn_ln2_b': (0.0, 0.1)}
    factors = {'L0_gnn_att_dst1': 4.136, 'L0_gnn_att_src2': 6.608, 'L0_gnn_att_dst2': 8.0}
    for name, (base, spread) in spreads.items():
        noise = np.random.default_rng([zlib.crc32(name.encode()), seed]).standard_normal(out[name].shape)
        drawn = base * np.exp(spread * noise) if base else spread * noise
        out[name] = jnp.asarray(drawn.astype(out[name].dtype))
    for name, factor in factors.items():
        out[name] = (out[name] * factor).astype(out[name].dtype)
    return out
```

```python
import numpy as np
import concourse.bass as bass
from concourse import mybir
from contextlib import ExitStack

N = 1250
P = 125
T = N // P
D = 768
KD = D // 128
HALF = D // 2
EDGES = 41250
H = 12
HD = D // H
VW = HD + 1
NE = 8
FF = 384
KF = FF // 128
EPS = 1e-5
SLOPE = 0.2
FAR = 1e30
CHUNKS = [(0, 418), (418, 416), (834, 416)]
GQ = 250
NG = N // GQ
BANK = 512

EROWS = -(-EDGES // 128)
LEAD = 3
ECOLS = LEAD + 3 * 128
ALL_STEPS = 1 + LEAD + EROWS + (-(1 + LEAD + EROWS)) % 4
STRIDE = 32
NEAR_STEPS = 40
WINDOW = NEAR_STEPS - 1


class Order:

    def __init__(self, eng, sem):
        self.eng, self.sem, self.base, self.turn, self.n = eng, sem, 0, 0, 0

    def did(self, ins):
        ins.then_inc(self.sem, 1)
        self.n += 1

    def wait(self):
        self.eng.wait_ge(self.sem, self.turn + (self.base + self.n))

    def loop(self, i, per):
        self.base, self.n, self.turn, self.per = self.base + self.n, 0, i * per, per

    def end(self, turns):
        assert self.n == self.per, (self.n, self.per)
        self.base, self.n, self.turn = self.base + turns * self.per, 0, 0


def build(nc, x, src, dst, gw1, gas1, gad1, gb1, gw2, gas2, gad2, gb2,
          wqkv, wproj, wrouter, w1, w2, ln1g, ln1b, ln2g, ln2b, out):
    f32, f32r, bf16, f16 = mybir.dt.float32, mybir.dt.float32r, mybir.dt.bfloat16, mybir.dt.float16
    i32, u32, u16 = mybir.dt.int32, mybir.dt.uint32, mybir.dt.uint16
    ALU, ACT, AX = mybir.AluOpType, mybir.ActivationFunctionType, mybir.AxisListType
    size = {f32: 4, f32r: 4, bf16: 2, f16: 2, i32: 4, u32: 4, u16: 2}
    ds = bass.ds

    hid_d = nc.dram_tensor("hid_d", (N, D), f32).ap()
    x1_d = nc.dram_tensor("x1_d", (N, D), f32).ap()
    xa_d = nc.dram_tensor("xa_d", (N, D), f32).ap()
    xn_d = nc.dram_tensor("xn_d", (N, D), f32).ap()
    o_d = nc.dram_tensor("o_d", (N, D), f32).ap()

    base = (nc.sbuf_base + 63) // 64 * 64
    top = [0]

    def put(name, shape, dt, at=None):
        n = int(np.prod(shape[1:])) * size[dt]
        n = (n + 31) // 32 * 32
        if at is None:
            at = top[0]
            top[0] += n
        put.end = at + n
        assert base + put.end <= nc.sbuf_usable_end, (name, put.end)
        return nc.alloc_sbuf_tensor_at(name, shape, dt, offset=base + at)

    ident = put("ident", [128, 128], f32)
    ones = put("ones", [P, P], f32)
    flag = put("flag", [1, 2], i32)
    bn = put("bn", [P, 2, 12], f32)
    stat = put("stat", [P, 2, 8], f32)
    es = put("es", [P, T], f32)
    ed = put("ed", [P, T], f32)
    ed02 = put("ed02", [P, T], f32)
    zsum = put("zsum", [P, 2, 8], f32)
    lnc = put("lnc", [P, T, 6], f32)
    mcol = put("mcol", [P, 2, T], f32)
    rz = put("rz", [P, 2, 2], f32)
    gate = put("gate", [P, T, NE], f32)
    FREE = top[0]

    att = put("att", [P, 2, D], f32)
    brow = put("brow", [P, D], f32)
    WAT = top[0]
    whi = put("whi", [128, KD, D], f32r)
    wlo = put("wlo", [128, KD, D], f32r)
    hhi = put("hhi", [P, T, D], f32r)
    HLO = top[0]
    hlo = put("hlo", [P, T, D], f32r)
    xall = put("xall", [P, T, D], f32, at=HLO)
    cnt = put("cnt", [P, T, N], u16)
    far = put("far", [P, T, N], bf16)
    esb = put("esb", [P, N], f32)
    LAT = top[0]
    lg2 = put("lg2", [P, 2, N], f32)
    cand = put("cand", [P, N], bf16)
    tin = put("tin", [P, 2, D], f32)
    wst = put("wst", [128, 2, D], f32)
    PTAT = top[0]
    pthi = put("pthi", [P, 2, N], f32r)
    ptlo = put("ptlo", [P, 2, N], f32r)
    txhi = put("txhi", [128, 2, D - 18], f32r, at=PTAT)
    txlo = put("txlo", [128, 2, D - 18], f32r, at=put.end)
    xres = put("xres", [P, 2, D], f32, at=WAT)
    xab = put("xab", [P, 2, D], f32, at=put.end)
    xnb = put("xnb", [P, 2, D], f32, at=put.end)
    lnrow = put("lnrow", [P, 2, D], f32, at=put.end)
    ohs = put("ohs", [128, 4, N], f16, at=LAT)
    ohd = put("ohd", [128, 4, P], f16, at=PTAT)
    iota = put("iota", [128, N], f16, at=put.end)
    edge = put("edge", [128, 2, ECOLS], f32, at=put.end)
    selfc = put("selfc", [128, T], f32, at=put.end)
    eraw = put("eraw", [128, 2, 3, 128], i32, at=put.end)
    efl = put("efl", [128, 2, 3, 128], f32, at=put.end)
    lohi = put("lohi", [128, 2, ECOLS], f32, at=put.end)
    viol = put("viol", [128, 4], f32, at=put.end)
    GRAPH_TOP = top[0]

    XT = FREE
    xthi = put("xthi", [128, KD, N], f32r, at=XT)
    xtlo = put("xtlo", [128, KD, N], f32r, at=put.end)
    VAT = put.end
    val = put("val", [P, T, H, VW], f32, at=VAT)
    HEADS = put.end
    qst = put("qst", [128, 2, N], f32r, at=HEADS)
    q2 = put("q2", [128, 2, N], f32r, at=put.end)
    kst = put("kst", [128, 2, N], f32r, at=put.end)
    k2 = put("k2", [128, 2, N], f32r, at=put.end)
    raw = put("raw", [128, 2, N], f32, at=put.end)
    wqhi = put("wqhi", [128, 2, KD, 128], f32r, at=put.end)
    wqlo = put("wqlo", [128, 2, KD, 128], f32r, at=put.end)
    wqst = put("wqst", [128, 2, KD, 128], f32, at=put.end)
    prob = put("prob", [P, 2, T, GQ], f32, at=put.end)
    obuf = put("obuf", [P, 2, 2, HD], f32, at=put.end)
    wvhi = put("wvhi", [128, KD, D], f32r, at=HEADS)
    wvlo = put("wvlo", [128, KD, D], f32r, at=put.end)
    wvst = put("wvst", [128, 2, D], f32, at=put.end)
    vtin = put("vtin", [P, 2, D], f32, at=put.end)
    vxhi = put("vxhi", [128, 2, D - 18], f32r, at=put.end)
    vxlo = put("vxlo", [128, 2, D - 18], f32r, at=put.end)
    wphi = put("wphi", [128, KD, D], f32r, at=XT)
    wplo = put("wplo", [128, KD, D], f32r, at=put.end)
    oxhi = put("oxhi", [128, 2, D - 18], f32r, at=put.end)
    oxlo = put("oxlo", [128, 2, D - 18], f32r, at=put.end)
    acc = put("acc", [P, T, D], f32, at=VAT)
    XT2 = put.end
    yhi = put("yhi", [128, KD, N], f32r, at=XT2)
    ylo = put("ylo", [128, KD, N], f32r, at=put.end)
    XN2 = put.end
    xn2 = put("xn2", [P, T, D], f32, at=XN2)
    row2 = put("row2", [P, 2, D], f32, at=put.end)
    otin = put("otin", [P, 2, D], f32, at=put.end)
    xain = put("xain", [P, 2, D], f32, at=put.end)
    x1in = put("x1in", [P, 2, D], f32, at=XT2)
    wpst = put("wpst", [128, 2, D], f32, at=put.end)
    w1hi = put("w1hi", [128, KD, FF], f32r, at=XT)
    w1lo = put("w1lo", [128, KD, FF], f32r, at=put.end)
    w2hi = put("w2hi", [128, KF, D], f32r, at=put.end)
    w2lo = put("w2lo", [128, KF, D], f32r, at=put.end)
    w1st = put("w1st", [128, KD, FF], f32, at=put.end)
    w2st = put("w2st", [128, KF, D], f32, at=put.end)
    assert put.end <= VAT
    hthi = put("hthi", [128, KF, N], f32r, at=XN2)
    htlo = put("htlo", [128, KF, N], f32r, at=put.end)
    gel = put("gel", [128, 3, CHUNKS[0][1]], f32, at=put.end)
    wrhi = put("wrhi", [128, KD, NE], f32r, at=put.end)
    wrlo = put("wrlo", [128, KD, NE], f32r, at=put.end)
    wrst = put("wrst", [128, KD, NE], f32, at=put.end)
    logt = put("logt", [NE, N], f32, at=put.end)
    logit = put("logit", [P, T, NE], f32, at=put.end)
    top8 = put("top8", [P, T, 8], f32, at=put.end)
    ix8 = put("ix8", [P, T, 8], u32, at=put.end)
    ixf = put("ixf", [P, T, 2], f32, at=put.end)
    iota8 = put("iota8", [P, NE], f32, at=put.end)
    hot = put("hot", [P, 2, T, NE], f32, at=put.end)
    gcol = put("gcol", [P, T, 4], f32, at=put.end)

    ctx = ExitStack()
    with ctx:
        ps = ctx.enter_context(nc.psum_tensor("ps", [128, 8 * BANK], f32))
        sems = {}

        def sem(name):
            if name not in sems:
                sems[name] = ctx.enter_context(nc.semaphore(name))
            return sems[name]

        def bank(b, rows=128, cols=BANK):
            return ps[0:rows, b * BANK:b * BANK + cols]

        def two(b, rows, cols):
            return ps[0:rows, b * BANK:(b + 2) * BANK].rearrange("p (a c) -> p a c", a=2)[:, :, 0:cols]

        def halves(ap):
            return ap.rearrange("p (a c) -> p a c", a=2)

        ENGINES = ("tensor", "vector", "scalar", "gpsimd", "sync")

        def alone(eng):
            eng.sem_inc(sem("passed"), 1)

        def leave(eng, name):
            eng.drain().then_inc(sem(f"left_{name}"), 1)

        def enter(eng, name, phase, others=ENGINES):
            for o in others:
                if o != name:
                    eng.wait_ge(sem(f"left_{o}"), phase)

        def three(pe, o, lhi, llo, rhi, rlo, start, stop):
            pe.matmul(o, lhi, rhi, start=start, stop=False)
            pe.matmul(o, llo, rhi, start=False, stop=False)
            return pe.matmul(o, lhi, rlo, start=False, stop=stop)

        def load_split_sp(sp, n, dram, stage):
            for k in range(KD):
                if k >= 2:
                    sp.wait_ge(sem("w_lo"), KD * n + k - 1)
                sp.dma_start(stage[:, k % 2, :], dram[k * 128:(k + 1) * 128, :]).then_inc(sem(f"w_in{k % 2}"), 16)

        def split_act(act, n, stage, hi):
            for k in range(KD):
                act.wait_ge(sem(f"w_in{k % 2}"), 16 * (KD // 2 * n + k // 2 + 1))
                act.activation(hi[:, k, :], stage[:, k % 2, :], ACT.Copy).then_inc(sem("w_hi"), 1)

        def split_pool(pool, n, stage, hi, lo):
            for k in range(KD):
                pool.wait_ge(sem("w_hi"), KD * n + k + 1)
                pool.tensor_tensor(lo[:, k, :], stage[:, k % 2, :], hi[:, k, :].bitcast(f32), ALU.subtract)\
                    .then_inc(sem("w_lo"), 1)

        def gemm_pe(pe, n, source, ready, hi, lo, whi_, wlo_):

            def transposes(t, u):
                ready(t, u)
                pe.wait_ge(sem("tile_lo"), t + (T * n + 1))
                tile = source(t, u)
                for k in range(KD):
                    last = pe.transpose(ps[:, (2 * u + k // 3) * BANK + k % 3 * P:(2 * u + k // 3) * BANK + (k % 3 + 1) * P],
                                        tile[:, k * 128:(k + 1) * 128], ident[0:P, 0:P])
                last.then_inc(sem("tile_raw"), 1)

            def product(t, u):
                pe.wait_ge(sem("tile_lo"), t + (T * n + 3))
                pe.wait_ge(sem("tile_yfree"), t + (T * n + 1))
                for h in range(2):
                    for k in range(KD):
                        last = three(pe, bank(4 + 2 * u + h, P, HALF), hi[:, u, k * P:(k + 1) * P],
                                     lo[:, u, k * P:(k + 1) * P], whi_[:, k, h * HALF:(h + 1) * HALF],
                                     wlo_[:, k, h * HALF:(h + 1) * HALF], k == 0, k == KD - 1)
                last.then_inc(sem("tile_y"), 1)

            transposes(0, 0)
            with pe.Fori(0, T // 2 - 1) as i:
                transposes(2 * i + 1, 1)
                product(2 * i, 0)
                transposes(2 * i + 2, 0)
                product(2 * i + 1, 1)
            transposes(T - 1, 1)
            product(T - 2, 0)
            product(T - 1, 1)

        def gemm_hi(act, n, hi, t, u):
            act.wait_ge(sem("tile_raw"), t + (T * n + 3))
            act.wait_ge(sem("tile_y"), t + (T * n + 1))
            act.activation(halves(hi[:, u, :]), two(2 * u, 128, 3 * P), ACT.Copy).then_inc(sem("tile_hi"), 1)

        def gemm_lo(dve, n, hi, lo, t, u):
            dve.wait_ge(sem("tile_hi"), t + (T * n + 1))
            dve.tensor_tensor(halves(lo[:, u, :]), two(2 * u, 128, 3 * P), halves(hi[:, u, :]).bitcast(f32),
                              ALU.subtract).then_inc(sem("tile_lo"), 1)

        def ring_sp(sp, n, dram, ring):
            with sp.Fori(0, T // 2) as i:
                for u in range(2):
                    sp.wait_ge(sem("tile_raw"), 2 * i + (T * n + u + 1))
                    sp.dma_start(ring[:, u, :], dram.rearrange("(t p) d -> p t d", p=P)[:, ds(2 * i + u, 1), :])\
                        .then_inc(sem(f"tile_in{u}"), 16)

        def scores_dve(dve, n, i, u):
            t = 2 * i + u
            y = two(4 + 2 * u, P, HALF)
            dve.wait_ge(sem("tile_y"), t + (T * n + 3))
            dve.wait_ge(sem("tile_yhi"), t + (T * n + 1))
            dve.wait_ge(sem("tile_yfree"), t + (T * n + 2))
            for a, col in ((0, es), (1, ed)):
                dve.scalar_tensor_tensor(halves(lg2[:, a, 0:D]), y, 1.0, halves(att[:, a, :]), ALU.mult, ALU.mult,
                                         accum_out=col[:, ds(t, 1)])
            dve.tensor_tensor(halves(hlo[:, ds(t, 1), :].rearrange("p o d -> p (o d)")), y,
                              halves(hhi[:, ds(t, 1), :].rearrange("p o d -> p (o d)")).bitcast(f32), ALU.subtract)\
                .then_inc(sem("tile_yfree"), 1)

        def scores_act(act, n, i, u):
            t = 2 * i + u
            act.wait_ge(sem("tile_y"), t + (T * n + 3))
            act.activation(halves(hhi[:, ds(t, 1), :].rearrange("p o d -> p (o d)")), two(4 + 2 * u, P, HALF), ACT.Copy)\
                .then_inc(sem("tile_yhi"), 1)

        def h_phase_dve(dve, n):
            gemm_lo(dve, n, txhi, txlo, 0, 0)
            with dve.Fori(0, T // 2 - 1) as i:
                gemm_lo(dve, n, txhi, txlo, 2 * i + 1, 1)
                scores_dve(dve, n, i, 0)
                gemm_lo(dve, n, txhi, txlo, 2 * i + 2, 0)
                scores_dve(dve, n, i, 1)
            gemm_lo(dve, n, txhi, txlo, T - 1, 1)
            scores_dve(dve, n, T // 2 - 1, 0)
            scores_dve(dve, n, T // 2 - 1, 1)

        def h_phase_act(act, n, row=None):
            row = row or (lambda t, u: None)
            row(0, 0)
            row(1, 1)
            gemm_hi(act, n, txhi, 0, 0)
            with act.Fori(0, T // 2 - 1) as i:
                gemm_hi(act, n, txhi, 2 * i + 1, 1)
                row(2 * i + 2, 0)
                scores_act(act, n, i, 0)
                gemm_hi(act, n, txhi, 2 * i + 2, 0)
                row(2 * i + 3, 1)
                scores_act(act, n, i, 1)
            gemm_hi(act, n, txhi, T - 1, 1)
            scores_act(act, n, T // 2 - 1, 0)
            scores_act(act, n, T // 2 - 1, 1)

        def diag_dve(dve, n):
            dve.wait_ge(sem("tile_yfree"), T * (n + 1) + 2)
            dve.tensor_scalar(ed02[:, :], ed[:, :], SLOPE, None, ALU.mult)
            dve.tensor_tensor(lg2[:, 0, :].rearrange("p (t c) -> p t c", t=T),
                              ident[0:P, 0:P].rearrange("p (o c) -> p o c", o=1).broadcast_to([P, T, P]),
                              es[:, :].rearrange("p (t o) -> p t o", o=1).broadcast_to([P, T, P]), ALU.mult)\
                .then_inc(sem("agg_diag"), 1)

        def agg_pe(pe, n):
            pe.wait_ge(sem("agg_diag"), n + 1)
            for b, c in ((0, 500), (1, 500), (2, 250)):
                last = pe.matmul(bank(b, P, c), ones[:, :], lg2[:, 0, 500 * b:500 * b + c], start=True, stop=True)
            last.then_inc(sem("agg_esb_raw"), 1)

            def transposes(t, u):
                pe.wait_ge(sem("agg_w"), t + (T * n + 1))
                pe.wait_ge(sem("agg_lo"), t + (T * n + 1))
                for s in range(T):
                    at = (s // 4) * BANK + s % 4 * P
                    last = pe.transpose(ps[0:P, at:at + P], lg2[:, u, s * P:(s + 1) * P], ident[0:P, 0:P])
                last.then_inc(sem("agg_raw"), 1)

            def sums(t, u):
                pe.wait_ge(sem("agg_lo"), t + (T * n + 2))
                pe.wait_ge(sem("agg_read"), t + (T * n + 1))
                for h in range(2):
                    for s in range(T):
                        last = three(pe, bank(3 + 2 * u + h, P, HALF), pthi[:, u, s * P:(s + 1) * P],
                                     ptlo[:, u, s * P:(s + 1) * P], hhi[:, s, h * HALF:(h + 1) * HALF],
                                     hlo[:, s, h * HALF:(h + 1) * HALF], s == 0, s == T - 1)
                last.then_inc(sem("agg_sum"), 1)

            transposes(0, 0)
            with pe.Fori(0, T // 2 - 1) as i:
                transposes(2 * i + 1, 1)
                sums(2 * i, 0)
                transposes(2 * i + 2, 0)
                sums(2 * i + 1, 1)
            transposes(T - 1, 1)
            sums(T - 2, 0)
            sums(T - 1, 1)

        def agg_pool(pool, n, extra=None):
            pool.wait_ge(sem("agg_esb"), 2 * n + 2)

            def candidates(t):
                pool.wait_ge(sem("agg_maxed"), t + (T * n + 1))
                alone(pool)
                pool.tensor_tensor(cand[:, :], esb[:, :], far[:, ds(t, 1), :].rearrange("p o n -> p (o n)"),
                                   ALU.subtract).then_inc(sem("agg_cand"), 1)

            candidates(0)
            candidates(1)
            with pool.Fori(0, T // 2 - 1) as i:
                for v in range(2):
                    candidates(2 * i + 2 + v)
                    if extra:
                        extra(2 * i + v, v)
            if extra:
                extra(T - 2, 0)
                extra(T - 1, 1)

        def agg_act(act, n, extra=None):
            act.wait_ge(sem("agg_esb_raw"), n + 1)
            act.activation(halves(esb[:, 0:1000]), two(0, P, 500), ACT.Copy).then_inc(sem("agg_esb"), 1)
            act.activation(esb[:, 1000:N], bank(2, P, 250), ACT.Copy).then_inc(sem("agg_esb"), 1)
            act.wait_ge(sem("agg_esb"), 2 * n + 2)

            def sloped(t, u):
                act.wait_ge(sem("agg_raw"), t + (T * n + 1))
                act.activation(lg2[:, u, :], esb[:, :], ACT.Identity, scale=SLOPE, bias=ed02[:, ds(t, 1)])\
                    .then_inc(sem("agg_sl"), 1)

            def step(t, u, more, done=None):
                act.wait_ge(sem("agg_l"), t + (T * n + 1))
                act.activation(lg2[:, u, :], lg2[:, u, :], ACT.Exp, bias=zsum[:, u, 0:1]).then_inc(sem("agg_e"), 1)
                act.wait_ge(sem("agg_raw"), t + (T * n + 3))
                act.wait_ge(sem("agg_sum"), t + (T * n + 1))
                act.activation(halves(pthi[:, u, 0:1000]), two(0, P, 500), ACT.Copy).then_inc(sem("agg_hi"), 1)
                act.activation(pthi[:, u, 1000:N], bank(2, P, 250), ACT.Copy).then_inc(sem("agg_hi"), 1)
                if more:
                    sloped(t + 1, 1 - u)
                if done is not None and extra:
                    extra(done, 1 - u)

            sloped(0, 0)
            step(0, 0, True)
            with act.Fori(0, T // 2 - 1) as i:
                step(2 * i + 1, 1, True, 2 * i)
                step(2 * i + 2, 0, True, 2 * i + 1)
            step(T - 1, 1, False, T - 2)
            if extra:
                extra(T - 1, 1)

        def agg_dve(dve, order, n, finish, finish_steps):
            def maximum(t, u):
                dve.wait_ge(sem("agg_cand"), t + (T * n + 1))
                order.did(dve.tensor_reduce(zsum[:, u, 2:3], cand[:, :], AX.X, ALU.max))
                order.wait()
                dve.sem_inc(sem("agg_maxed"), 1)
                order.did(dve.tensor_scalar(zsum[:, u, 3:4], zsum[:, u, 2:3], ed[:, ds(t, 1)], -1.0, ALU.add, ALU.mult))
                order.wait()
                dve.scalar_tensor_tensor(zsum[:, u, 0:1], zsum[:, u, 3:4], SLOPE, zsum[:, u, 3:4], ALU.mult, ALU.min)\
                    .then_inc(sem("agg_m"), 1)

            def leaky(t, u):
                dve.wait_ge(sem("agg_sl"), t + (T * n + 1))
                dve.wait_ge(sem("agg_m"), t + (T * n + 1))
                dve.scalar_tensor_tensor(lg2[:, u, :], esb[:, :], ed[:, ds(t, 1)], lg2[:, u, :], ALU.add, ALU.max)\
                    .then_inc(sem("agg_l"), 1)

            def weigh(t, u):
                dve.wait_ge(sem("agg_e"), t + (T * n + 1))
                dve.scalar_tensor_tensor(lg2[:, u, :], lg2[:, u, :], 1.0,
                                         cnt[:, ds(t, 1), :].rearrange("p o n -> p (o n)"), ALU.mult, ALU.mult,
                                         accum_out=zsum[:, u, 4:5]).then_inc(sem("agg_w"), 1)

            def lower(t, u):
                dve.wait_ge(sem("agg_hi"), 2 * t + (2 * T * n + 2))
                dve.tensor_tensor(halves(ptlo[:, u, 0:1000]), two(0, P, 500), halves(pthi[:, u, 0:1000]).bitcast(f32), ALU.subtract)
                dve.tensor_tensor(ptlo[:, u, 1000:N], bank(2, P, 250), pthi[:, u, 1000:N].bitcast(f32), ALU.subtract)\
                    .then_inc(sem("agg_lo"), 1)

            def ending(t, u):
                dve.wait_ge(sem("agg_w"), t + (T * n + 1))
                order.did(dve.reciprocal(zsum[:, u, 5:6], zsum[:, u, 4:5]))
                dve.wait_ge(sem("agg_sum"), t + (T * n + 3))
                order.wait()
                finish(t, u)

            def step(t, u, more, done):
                leaky(t, u)
                if more:
                    maximum(t + 1, 1 - u)
                weigh(t, u)
                lower(t, u)
                if done is not None:
                    ending(done, 1 - u)

            maximum(0, 0)
            step(0, 0, True, None)
            with dve.Fori(0, T // 2 - 1) as i:
                order.loop(i, 2 * (2 + 1 + finish_steps))
                step(2 * i + 1, 1, True, 2 * i)
                step(2 * i + 2, 0, True, 2 * i + 1)
            order.end(T // 2 - 1)
            step(T - 1, 1, False, T - 2)
            ending(T - 1, 1)

        def attention_pe(pe):
            pe.sem_inc(sem("st"), 1)
            pe.sem_inc(sem("pv"), 2)

            def project(p):
                pe.wait_ge(sem("wq_lo"), p + 2)
                if not isinstance(p, int):
                    pe.wait_ge(sem("m_set"), 4 * p)
                for m in range(2):
                    for c, (at, n) in enumerate(CHUNKS):
                        if m:
                            pe.wait_ge(sem("raw_set"), 6 * p + c + 1)
                        for k in range(KD):
                            last = three(pe, bank(c, 128, n), wqhi[:, m, k, :], wqlo[:, m, k, :],
                                         xthi[:, k, at:at + n], xtlo[:, k, at:at + n], k == 0, k == KD - 1)
                        last.then_inc(sem("qk_raw"), 1)

            def rough(p, e, t):
                r = 64 * e
                if t == 0:
                    pe.wait_ge(sem("qk_split"), 2 * p + e + 1)
                    pe.wait_ge(sem("raw_set"), 6 * p + 6)
                    if e == 1:
                        pe.wait_ge(sem("m_set"), 4 * p + 2)
                else:
                    pe.wait_ge(sem("max"), 20 * p + 10 * e + t)
                for c, (a, b) in enumerate(((0, 512), (512, 1024), (1024, N))):
                    last = pe.matmul(bank(c, P, b - a), qst[r:r + 64, e, t * P:(t + 1) * P],
                                     kst[r:r + 64, e, a:b], start=True, stop=True)
                last.then_inc(sem("rough"), 1)

            def maxima(p, e):
                pe.wait_ge(sem("max"), 20 * p + 10 * e + T)
                for t in range(T):
                    at = (t // 4) * BANK + t % 4 * P
                    last = pe.transpose(ps[0:1, at:at + P], mcol[:, e, t:t + 1], ident[0:P, 0:P])
                last.then_inc(sem("m_raw"), 1)

            def weighted(p, e, g, part):
                n = 2 * NG * p + NG * e + g
                if part == 0:
                    pe.wait_ge(sem("exp"), 50 * p + (25 * e + 5 * g + 5 + 3))
                    pe.wait_ge(sem("o_row"), n + 1)
                for j in range(4 * part, 4 * part + 4):
                    q, kt = j // T, j % T
                    slot = (NG * e + g) % 2
                    last = pe.matmul(ps[0:P, (6 + slot) * BANK + q * VW:(6 + slot) * BANK + (q + 1) * VW],
                                     prob[:, slot, kt, q * P:(q + 1) * P],
                                     val[:, kt, ds(2 * p + e, 1), :].rearrange("p o c -> p (o c)"),
                                     start=kt == 0, stop=kt == T - 1)
                if part == 4:
                    last.then_inc(sem("pv"), 1)

            PLACES = {1: (1, 3), 2: (0, 2, 4), 3: (0, 2, 4), 4: (1, 3)}

            def head(p, e, other):
                pe.wait_ge(sem("m_set"), 4 * p + 2 * e + 2)
                pe.wait_ge(sem("qk_split"), 2 * p + e + 1)
                pe.wait_ge(sem("kst_set"), 2 * p + e + 1)
                t = 0
                for g in range(NG):
                    for kp in range(5):
                        j = 5 * g + kp
                        b = 3 + j % 3
                        before = {0: 3, 1: 1, 2: 2}.get(j, j + 1)
                        pe.wait_ge(sem("exp"), 50 * p + (25 * e + before))
                        for z in range(2):
                            kt = 2 * kp + z
                            o = ps[0:P, b * BANK + z * GQ:b * BANK + (z + 1) * GQ]
                            pe.matmul(o, kst[:, e, kt * P:(kt + 1) * P], qst[:, e, g * GQ:(g + 1) * GQ],
                                      start=True, stop=False)
                            last = pe.matmul(o, k2[:, e, kt * P:(kt + 1) * P], q2[:, e, g * GQ:(g + 1) * GQ],
                                             start=False, stop=True)
                        last.then_inc(sem("st"), 1)
                        if g > 0:
                            weighted(p, e, g - 1, kp)
                        if other is not None and kp in PLACES.get(g, ()):
                            rough(*other, t)
                            t += 1
                if other is not None:
                    maxima(*other)
                for part in range(5):
                    weighted(p, e, NG - 1, part)

            def pair(p, last):
                head(p, 0, (p, 1))
                if not last:
                    project(p + 1)
                    head(p, 1, (p + 1, 0))
                else:
                    head(p, 1, None)

            pe.wait_ge(sem("heads_clear"), 1)
            project(0)
            for t in range(T):
                rough(0, 0, t)
            maxima(0, 0)
            with pe.Fori(0, H // 2 - 1) as p:
                pair(p, False)
            pair(H // 2 - 1, True)

        def attention_act(act):
            def split_qk(p):
                act.wait_ge(sem("wq_in"), 32 * p + 32)
                if not isinstance(p, int):
                    act.wait_ge(sem("qk_raw"), 6 * p)
                act.activation(wqhi[:, :, :, :].rearrange("p m k c -> p (m k c)"),
                               wqst[:, :, :, :].rearrange("p m k c -> p (m k c)"), ACT.Copy).then_inc(sem("wq_hi"), 1)

            def set_raw(p):
                if not isinstance(p, int):
                    act.wait_ge(sem("qk_split"), 2 * p)
                for m in range(2):
                    for c, (at, n) in enumerate(CHUNKS):
                        act.wait_ge(sem("qk_raw"), 6 * p + 3 * m + c + 1)
                        act.activation(raw[:, m, at:at + n], bank(c, 128, n), ACT.Copy).then_inc(sem("raw_set"), 1)

            def set_k(p, e):
                r = 64 * e
                act.wait_ge(sem("raw_set"), 6 * p + 6)
                act.wait_ge(sem("q_hi"), 2 * p + e + 1)
                act.activation(kst[64 - r:128 - r, e, :], raw[r:r + 64, 1, :], ACT.Copy)
                act.activation(q2[r:r + 64, e, :], qst[r:r + 64, e, :].bitcast(f32), ACT.Copy).then_inc(sem("kst_set"), 1)

            def set_m(p, e):
                r = 64 * (1 - e)
                act.wait_ge(sem("m_raw"), 2 * p + e + 1)
                act.activation(halves(q2[r:r + 1, e, 0:1000]), two(0, 1, 500), ACT.Copy).then_inc(sem("m_set"), 1)
                act.activation(q2[r:r + 1, e, 1000:N], bank(2, 1, 250), ACT.Copy).then_inc(sem("m_set"), 1)

            def exps(p, e):
                for g in range(NG):
                    slot = (NG * e + g) % 2
                    act.wait_ge(sem("pv"), 2 * NG * p + (NG * e + g + 1))
                    for kp in range(5):
                        j = 5 * g + kp
                        act.wait_ge(sem("st"), 50 * p + (25 * e + j + 2))
                        act.activation(prob[:, slot, 2 * kp:2 * kp + 2, :].rearrange("p k q -> p (k q)"),
                                       bank(3 + j % 3, P, 2 * GQ), ACT.Exp, scale=float(HD) ** -0.5)\
                            .then_inc(sem("exp"), 1)

            def pair(p, last):
                set_k(p, 1)
                if not last:
                    split_qk(p + 1)
                exps(p, 0)
                set_m(p, 1)
                if not last:
                    set_raw(p + 1)
                    set_k(p + 1, 0)
                exps(p, 1)
                if not last:
                    set_m(p + 1, 0)

            act.sem_inc(sem("exp"), 3)
            split_qk(0)
            set_raw(0)
            set_k(0, 0)
            set_m(0, 0)
            with act.Fori(0, H // 2 - 1) as p:
                pair(p, False)
            pair(H // 2 - 1, True)

        def attention_dve(dve, order):
            dve.sem_inc(sem("o_row"), 2)
            dve.wait_ge(sem("heads_clear"), 1)

            def split(p, e):
                r = 64 * e
                dve.wait_ge(sem("raw_set"), 6 * p + 6)
                if not isinstance(p, int) or p > 0:
                    dve.wait_ge(sem("st"), 50 * p + (25 * e - 24))
                dve.tensor_copy(qst[r:r + 64, e, :], raw[r:r + 64, 0, :]).then_inc(sem("q_hi"), 1)
                order.did(dve.tensor_copy(kst[r:r + 64, e, :], raw[r:r + 64, 1, :]))
                order.wait()
                dve.tensor_tensor(qst[64 - r:128 - r, e, :], raw[r:r + 64, 0, :], qst[r:r + 64, e, :].bitcast(f32), ALU.subtract)
                dve.tensor_tensor(k2[r:r + 64, e, :], raw[r:r + 64, 1, :], kst[r:r + 64, e, :].bitcast(f32), ALU.subtract)\
                    .then_inc(sem("qk_split"), 1)

            def maximum(p, e, t):
                dve.wait_ge(sem("rough"), 20 * p + (10 * e + t + 1))
                dve.tensor_reduce(mcol[:, e, t:t + 1], ps[0:P, 0:N], AX.X, ALU.max, negate=True).then_inc(sem("max"), 1)

            def outputs(p, e, g):
                c = NG * e + g
                slot = c % 2
                dve.wait_ge(sem("pv"), 2 * NG * p + (c + 3))
                dve.wait_ge(sem(f"o_out{slot}"), 16 * NG * p + 16 * (c // 2 + 1))
                o = ps[0:P, (6 + slot) * BANK:(6 + slot) * BANK + 2 * VW].rearrange("p (q c) -> p q c", q=2)
                order.did(dve.reciprocal(rz[:, slot, :].rearrange("p (q c) -> p q c", c=1), o[:, :, HD:VW]))
                order.wait()
                dve.tensor_tensor(obuf[:, slot, :, :], o[:, :, 0:HD],
                                  rz[:, slot, :].rearrange("p (q c) -> p q c", c=1).broadcast_to([P, 2, HD]), ALU.mult)\
                    .then_inc(sem("o_row"), 1)

            PLACES = {1: 2, 2: 3, 3: 3, 4: 2}

            def head(p, e, other):
                t = 0
                for g in range(NG):
                    if other is not None:
                        for _ in range(PLACES.get(g, 0)):
                            maximum(*other, t)
                            t += 1
                    if g > 0:
                        outputs(p, e, g - 1)
                outputs(p, e, NG - 1)

            def pair(p, last):
                split(p, 1)
                head(p, 0, (p, 1))
                if not last:
                    split(p + 1, 0)
                    head(p, 1, (p + 1, 0))
                else:
                    head(p, 1, None)

            split(0, 0)
            for t in range(T):
                maximum(0, 0, t)
            with dve.Fori(0, H // 2 - 1) as p:
                order.loop(p, 2 + 2 * NG)
                pair(p, False)
            order.end(H // 2 - 1)
            pair(H // 2 - 1, True)

        def experts_pe(pe):
            def expert(e):
                pe.wait_ge(sem("w1_lo"), e + 2)
                for c, (at, n) in enumerate(CHUNKS):
                    for f in range(KF):
                        j = KF * c + f
                        pe.wait_ge(sem("gelu"), 9 * e + (j + 1))
                        for k in range(KD):
                            last = three(pe, bank(j % 3, 128, n), w1hi[:, k, f * 128:(f + 1) * 128],
                                         w1lo[:, k, f * 128:(f + 1) * 128], yhi[:, k, at:at + n],
                                         ylo[:, k, at:at + n], k == 0, k == KD - 1)
                        last.then_inc(sem("hid"), 1)
                pe.wait_ge(sem("w2_lo"), e + 2)
                for t in range(T):
                    u = t % 2
                    c = next(c for c, (at, n) in enumerate(CHUNKS) if (t + 1) * P <= at + n)
                    pe.wait_ge(sem("ht"), 9 * e + KF * (c + 1))
                    pe.wait_ge(sem("added"), T * e + (t + 1))
                    for h in range(2):
                        for f in range(KF):
                            last = three(pe, bank(3 + 2 * u + h, P, HALF), hthi[:, f, t * P:(t + 1) * P],
                                         htlo[:, f, t * P:(t + 1) * P], w2hi[:, f, h * HALF:(h + 1) * HALF],
                                         w2lo[:, f, h * HALF:(h + 1) * HALF], f == 0, f == KF - 1)
                    last.then_inc(sem("ey"), 1)
            with pe.Fori(0, NE) as e:
                expert(e)

        block = ctx.enter_context(nc.Block())

        x_t = x.rearrange("(t p) d -> p t d", p=P)
        bcast = lambda v: v.rearrange("(o d) -> o d", o=1).broadcast_to([P, D])
        PH_EDGES, PH_H1, PH_G1, PH_H2, PH_G2, PH_V, PH_ATT, PH_O, PH_T, PH_R = range(1, 11)

        @block.sync
        def _(sp):
            sp.wait_ge(sem("eraw_clear"), 1)
            for a, e in ((0, src), (1, dst)):
                sp.dma_start(eraw[:, a, 0:2, :], e[0:256 * 128].rearrange("(c p k) -> p c k", c=2, p=128)).then_inc(sem("edges_in"), 16)
                full = EDGES // 128 - 256
                sp.dma_start(eraw[0:full, a, 2, :], e[256 * 128:(256 + full) * 128].rearrange("(p k) -> p k", p=full)).then_inc(sem("edges_in"), 16)
                sp.dma_start(eraw[full:full + 1, a, 2, 0:EDGES % 128],
                             e[(256 + full) * 128:EDGES].rearrange("(p k) -> p k", p=1)).then_inc(sem("edges_in"), 16)
            for g in range(2):
                sp.dma_start(xall[:, 5 * g:5 * g + 5, :], x_t[:, 5 * g:5 * g + 5, :]).then_inc(sem(f"x_in{g}"), 16)
            load_split_sp(sp, 0, gw1, wst)
            sp.dma_start(att[:, 0, :], bcast(gas1)).then_inc(sem("att_in"), 16)
            sp.dma_start(att[:, 1, :], bcast(gad1)).then_inc(sem("att_in"), 16)
            sp.dma_start(brow[:, :], bcast(gb1)).then_inc(sem("brow_in"), 16)
            leave(sp, "sync")
            leave(sp, "sync")
            enter(sp, "sync", PH_H1, ("tensor", "vector", "scalar"))
            sp.dma_start(att[:, 0, :], bcast(gas2)).then_inc(sem("att_in"), 16)
            sp.dma_start(att[:, 1, :], bcast(gad2)).then_inc(sem("att_in"), 16)
            sp.sem_inc(sem("g1_out0"), 16)
            sp.sem_inc(sem("g1_out1"), 16)
            with sp.Fori(0, T // 2) as i:
                for u in range(2):
                    sp.wait_ge(sem("g1_row"), 2 * i + u + 1)
                    sp.dma_start(hid_d.rearrange("(t p) d -> p t d", p=P)[:, ds(2 * i + u, 1), :], tin[:, u, :])\
                        .then_inc(sem(f"g1_out{u}"), 16)
            load_split_sp(sp, 1, gw2, wst)
            for u in range(2):
                sp.wait_ge(sem(f"g1_out{u}"), 16 * (T // 2 + 1))
            sp.dma_start(brow[:, :], bcast(gb2)).then_inc(sem("brow_in"), 16)
            leave(sp, "sync")
            ring_sp(sp, 1, hid_d, tin)
            leave(sp, "sync")
            enter(sp, "sync", PH_H2)
            sp.dma_start(lnrow[:, 0, :], bcast(ln1g)).then_inc(sem("lnrow_in"), 16)
            sp.dma_start(lnrow[:, 1, :], bcast(ln1b)).then_inc(sem("lnrow_in"), 16)
            for u in range(2):
                for n in ("x1", "xa", "xn"):
                    sp.sem_inc(sem(f"{n}_out{u}"), 16)
                sp.dma_start(xres[:, u, :], x_t[:, u, :]).then_inc(sem(f"xres_in{u}"), 16)
            def g2_rows(t, u, more):
                if more:
                    sp.wait_ge(sem("xres_free"), t + 1)
                    sp.dma_start(xres[:, u, :], x_t[:, ds(t + 2, 1), :]).then_inc(sem(f"xres_in{u}"), 16)
                for n, dram, buf in (("x1", x1_d, tin), ("xa", xa_d, xab), ("xn", xn_d, xnb)):
                    sp.wait_ge(sem(f"{n}_row"), t + 1)
                    sp.dma_start(dram.rearrange("(t p) d -> p t d", p=P)[:, ds(t, 1), :], buf[:, u, :])\
                        .then_inc(sem(f"{n}_out{u}"), 16)
            with sp.Fori(0, T // 2 - 1) as i:
                for u in range(2):
                    g2_rows(2 * i + u, u, True)
            for u in range(2):
                g2_rows(T - 2 + u, u, False)
            for u in range(2):
                for n in ("x1", "xa", "xn"):
                    sp.wait_ge(sem(f"{n}_out{u}"), 16 * (T // 2 + 1))
            leave(sp, "sync")
            enter(sp, "sync", PH_G2)
            load_split_sp(sp, 2, wqkv[:, 2 * D:3 * D], wvst)
            ring_sp(sp, 2, xn_d, vtin)
            leave(sp, "sync")
            enter(sp, "sync", PH_V)
            o_g = o_d.rearrange("(g q p) d -> p g q d", q=2, p=P)

            def load_qk(p):
                sp.wait_ge(sem("wq_lo"), p + 1)
                for m in range(2):
                    sp.dma_start(wqst[:, m, :, :], wqkv.rearrange("(k r) c -> r k c", r=128)[:, :, ds(m * D + p * 128, 128)])\
                        .then_inc(sem("wq_in"), 16)

            def store_o(p):
                for e in range(2):
                    for g in range(NG):
                        slot = (NG * e + g) % 2
                        sp.wait_ge(sem("o_row"), 2 * NG * p + (NG * e + g + 3))
                        sp.dma_start(o_g[:, g, :, ds(p * 128 + e * HD, HD)], obuf[:, slot, :, :])\
                            .then_inc(sem(f"o_out{slot}"), 16)
            for s in range(2):
                sp.sem_inc(sem(f"o_out{s}"), 16)
            load_qk(0)
            with sp.Fori(0, H // 2 - 1) as p:
                load_qk(p + 1)
                store_o(p)
            store_o(H // 2 - 1)
            for s in range(2):
                sp.wait_ge(sem(f"o_out{s}"), 16 * (NG * H // 2 + 1))
            leave(sp, "sync")
            enter(sp, "sync", PH_ATT)
            sp.dma_start(row2[:, 0, :], bcast(ln2g)).then_inc(sem("row2_in"), 16)
            sp.dma_start(row2[:, 1, :], bcast(ln2b)).then_inc(sem("row2_in"), 16)
            load_split_sp(sp, 3, wproj, wpst)
            with sp.Fori(0, T // 2) as i:
                for u in range(2):
                    for n, dram, ring, free, more in (("tile", o_d, otin, "tile_raw", 3 * T), ("xar", xa_d, xain, "xar_free", 0),
                                                      ("x1r", x1_d, x1in, "x1r_free", 0)):
                        sp.wait_ge(sem(free), 2 * i + (u + 1 + more))
                        sp.dma_start(ring[:, u, :], dram.rearrange("(t p) d -> p t d", p=P)[:, ds(2 * i + u, 1), :])\
                            .then_inc(sem(f"{n}_in{u}"), 16)
            leave(sp, "sync")
            enter(sp, "sync", PH_O)
            leave(sp, "sync")
            def load_w1(e):
                sp.wait_ge(sem("w1_lo"), e + 1)
                sp.dma_start(w1st[:, :, :], w1.rearrange("e (k r) f -> e r k f", r=128)[ds(e, 1), :, :, :]
                             .rearrange("o r k f -> (o r) k f")).then_inc(sem("w1_in"), 16)

            def load_w2(e):
                sp.wait_ge(sem("w2_lo"), e + 1)
                sp.dma_start(w2st[:, :, :], w2.rearrange("e (k r) f -> e r k f", r=128)[ds(e, 1), :, :, :]
                             .rearrange("o r k f -> (o r) k f")).then_inc(sem("w2_in"), 16)
            load_w1(0)
            load_w2(0)
            enter(sp, "sync", PH_T, ("tensor", "vector", "scalar"))
            sp.dma_start(wrst[:, :, :], wrouter.rearrange("(k r) e -> r k e", r=128)).then_inc(sem("wr_in"), 16)
            leave(sp, "sync")
            leave(sp, "sync")
            with sp.Fori(0, NE - 1) as e:
                load_w1(e + 1)
                load_w2(e + 1)
            for t in range(T):
                sp.wait_ge(sem("final"), t + 1)
                sp.dma_start(out.rearrange("(t p) d -> p t d", p=P)[:, t, :], acc[:, t, :]).then_inc(sem("out"), 16)
            sp.wait_ge(sem("out"), 16 * T)

        @block.gpsimd
        def _(pool):
            order = Order(pool, sem("pool_order"))
            pool.memset(eraw[:, :, :, :], -1).then_inc(sem("eraw_clear"), 1)
            order.did(pool.memset(ident[:, :], 0.0))
            order.did(pool.memset(ones[:, :], 1.0))
            order.did(pool.memset(edge[:, :, :], -1.0))
            order.did(pool.iota(iota[:, :], [[1, N]], base=0, channel_multiplier=0, allow_small_or_imprecise_dtypes=True))
            order.did(pool.iota(selfc[:, :], [[P, T]], base=0, channel_multiplier=1, allow_small_or_imprecise_dtypes=True))
            for j in range(T):
                start = 0 if j == 0 else STRIDE * (j - 1) + WINDOW
                end = STRIDE * j + WINDOW if j < T - 1 else ECOLS
                if start < end:
                    order.did(pool.memset(lohi[:, 0, start:end], float(P * j)))
                start, end = STRIDE * j, (STRIDE * (j + 1) if j < T - 1 else ECOLS)
                order.did(pool.memset(lohi[:, 1, start:end], float(P * (j + 1))))
            order.wait()
            order.did(pool.affine_select(out=ident[:, :], in_=ident[:, :], compare_op=ALU.not_equal, fill=1.0,
                                         base=0, pattern=[[-1, 128]], channel_multiplier=1))
            order.wait()
            pool.sem_inc(sem("consts"), 1)
            for t in range(T):
                pool.wait_ge(sem("ln_sum"), t + 1)
                pool.tensor_scalar(lnc[:, t, 1:2], lnc[:, t, 0:1], -1.0 / D, None, ALU.mult).then_inc(sem("ln_mean"), 1)
            pool.wait_ge(sem("ln_sq"), T)
            pool.tensor_scalar(lnc[:, :, 3:4], lnc[:, :, 2:3], 1.0 / D, EPS, ALU.mult, ALU.add).then_inc(sem("ln_var"), 1)
            split_pool(pool, 0, wst, whi, wlo)
            leave(pool, "gpsimd")
            leave(pool, "gpsimd")
            enter(pool, "gpsimd", PH_H1, ("tensor", "vector", "scalar"))
            agg_pool(pool, 0, None)
            split_pool(pool, 1, wst, whi, wlo)
            leave(pool, "gpsimd")
            leave(pool, "gpsimd")
            enter(pool, "gpsimd", PH_H2)

            def affine(t, u):
                pool.wait_ge(sem("xn_normed"), t + 1)
                pool.tensor_tensor(xnb[:, u, :], xnb[:, u, :], lnrow[:, 0, :], ALU.mult).then_inc(sem("xn_scaled"), 1)
                pool.wait_ge(sem("xn_scaled"), t + 1)
                pool.tensor_tensor(xnb[:, u, :], xnb[:, u, :], lnrow[:, 1, :], ALU.add).then_inc(sem("xn_row"), 1)
            pool.wait_ge(sem("lnrow_in"), 32)
            agg_pool(pool, 1, affine)
            leave(pool, "gpsimd")
            enter(pool, "gpsimd", PH_G2)
            order.did(pool.memset(val[:, :, :, HD:VW], 1.0))
            split_pool(pool, 2, wvst, wvhi, wvlo)
            pool.sem_inc(sem("v_copied"), 2)

            def whole(t, u):
                for part, tile, big in (("hi", vxhi, xthi), ("lo", vxlo, xtlo)):
                    if part == "hi":
                        pool.wait_ge(sem("tile_hi"), t + (2 * T + 1))
                    else:
                        pool.wait_ge(sem("tile_lo"), t + (2 * T + 3))
                    alone(pool)
                    last = pool.tensor_copy(big[:, :, ds(t * P, P)], tile[:, u, :].rearrange("p (k c) -> p k c", k=KD))
                last.then_inc(sem("v_copied"), 1)
            with pool.Fori(0, T // 2) as i:
                whole(2 * i, 0)
                whole(2 * i + 1, 1)
            leave(pool, "gpsimd")
            enter(pool, "gpsimd", PH_V)
            order.did(pool.memset(q2[:, :, :].bitcast(f32), 0.0))
            order.did(pool.memset(k2[:, :, :].bitcast(f32), 0.0))
            order.wait()
            order.did(pool.memset(k2[64:65, 0, :].bitcast(f32), 1.0))
            order.did(pool.memset(k2[0:1, 1, :].bitcast(f32), 1.0))
            order.wait()
            pool.sem_inc(sem("heads_clear"), 1)
            pool.sem_inc(sem("wq_lo"), 1)

            def split_qk(p):
                pool.wait_ge(sem("wq_hi"), p + 1)
                pool.tensor_tensor(wqlo[:, :, :, :], wqst[:, :, :, :], wqhi[:, :, :, :].bitcast(f32), ALU.subtract)\
                    .then_inc(sem("wq_lo"), 1)

            split_qk(0)
            with pool.Fori(0, H // 2 - 1) as p:
                split_qk(p + 1)
            leave(pool, "gpsimd")
            enter(pool, "gpsimd", PH_ATT)
            pool.sem_inc(sem("x1r_free"), 2)
            split_pool(pool, 3, wpst, wphi, wplo)
            pool.wait_ge(sem("row2_in"), 32)

            def second(t, u, i):
                xt_ = xn2[:, ds(t, 1), :].rearrange("p o d -> p (o d)")
                at_ = acc[:, ds(t, 1), :].rearrange("p o d -> p (o d)")
                pool.wait_ge(sem("n2_normed"), t + 1)
                alone(pool)
                pool.tensor_tensor(xt_, xt_, row2[:, 0, :], ALU.mult).then_inc(sem("n2_scaled"), 1)
                pool.wait_ge(sem(f"x1r_in{u}"), 16 * i + 16)
                alone(pool)
                pool.tensor_tensor(at_, at_, x1in[:, u, :], ALU.add).then_inc(sem("x1r_free"), 1)
                pool.wait_ge(sem("n2_scaled"), t + 1)
                alone(pool)
                pool.tensor_tensor(xt_, xt_, row2[:, 1, :], ALU.add).then_inc(sem("n2_row"), 1)
            with pool.Fori(0, T // 2) as i:
                second(2 * i, 0, i)
                second(2 * i + 1, 1, i)
            leave(pool, "gpsimd")
            enter(pool, "gpsimd", PH_O)
            pool.sem_inc(sem("w1_lo"), 1)
            pool.sem_inc(sem("w2_lo"), 1)

            def split_w(n, e, st, hi, lo):
                pool.wait_ge(sem(f"{n}_hi"), e + 1)
                pool.tensor_tensor(lo[:, :, :], st[:, :, :], hi[:, :, :].bitcast(f32), ALU.subtract)\
                    .then_inc(sem(f"{n}_lo"), 1)
            split_w("w1", 0, w1st, w1hi, w1lo)
            leave(pool, "gpsimd")
            enter(pool, "gpsimd", PH_T, ("tensor", "vector", "scalar"))
            pool.iota(iota8[:, :], [[1, NE]], base=0, channel_multiplier=0, allow_small_or_imprecise_dtypes=True)\
                .then_inc(sem("iota8"), 1)
            leave(pool, "gpsimd")
            with pool.Fori(0, NE - 1) as e:
                split_w("w2", e, w2st, w2hi, w2lo)
                split_w("w1", e + 1, w1st, w1hi, w1lo)
            split_w("w2", NE - 1, w2st, w2hi, w2lo)

        @block.tensor
        def _(pe):
            pe.wait_ge(sem("consts"), 1)
            pe.wait_ge(sem("edges_f"), 1)
            for a in range(2):
                for c in range(3):
                    last = pe.transpose(ps[:, a * BANK + c * 128:a * BANK + (c + 1) * 128], efl[:, a, c, :], ident[:, :])
            last.then_inc(sem("edges_t"), 1)
            pe.wait_ge(sem("viol"), 1)
            pe.matmul(ps[0:1, 2 * BANK:2 * BANK + 1], viol[:, 0:1], viol[:, 1:2], start=True, stop=True).then_inc(sem("viol_sum"), 1)
            pe.wait_ge(sem("flag"), 1)
            spread = pe.value_load(flag[0:1, 0:1], min_val=0, max_val=1)
            pe.sem_inc(sem("oh_free"), 4)
            pe.sem_inc(sem("tile_raw"), 2)
            pe.sem_inc(sem("tile_y"), 2)
            pe.sem_inc(sem("agg_raw"), 2)
            pe.sem_inc(sem("agg_sum"), 2)

            def count_edges(steps):
                turns = steps // 4
                with pe.Fori(0, T // 2) as jj:
                    for v in range(2):
                        pe.wait_ge(sem("block_read"), 2 * jj + v + 1)

                        def turn(r, first, last):
                            for u in range(4):
                                pe.wait_ge(sem("oh_ready"), (2 * jj + v) * steps + r * 4 + (u + 1))
                                for c, (a, b) in enumerate(((0, 512), (512, 1024), (1024, N))):
                                    mm = pe.matmul(ps[0:P, (3 * v + c) * BANK:(3 * v + c) * BANK + b - a],
                                                   ohd[:, u, :], ohs[:, u, a:b],
                                                   start=first and u == 0, stop=last and u == 3)
                                mm.then_inc(sem("oh_free"), 1)
                        turn(0, True, False)
                        with pe.Fori(1, turns - 1) as r:
                            turn(r, False, False)
                        turn(turns - 1, False, True)
                        pe.wait_ge(sem("oh_free"), (2 * jj + v + 1) * steps + 4)
                        pe.sem_inc(sem("block_done"), 1)
            with pe.If(spread == 0):
                count_edges(NEAR_STEPS)
            with pe.Else():
                count_edges(ALL_STEPS)
            leave(pe, "tensor")
            enter(pe, "tensor", PH_EDGES)

            def ready_x(t, u):
                pe.wait_ge(sem("h1_row"), t + 1)
            pe.wait_ge(sem("w_lo"), KD * 1)
            gemm_pe(pe, 0, lambda t, u: tin[:, u, :], ready_x, txhi, txlo, whi, wlo)
            leave(pe, "tensor")
            enter(pe, "tensor", PH_H1, ("vector", "scalar"))
            agg_pe(pe, 0)
            leave(pe, "tensor")
            enter(pe, "tensor", PH_G1)
            pe.wait_ge(sem("w_lo"), KD * 2)

            def slot_ready(m):
                def ready(t, u):
                    pe.wait_ge(sem(f"tile_in{u}"), 8 * t + (8 * T * m + 16 - 8 * u))
                return ready
            gemm_pe(pe, 1, lambda t, u: tin[:, u, :], slot_ready(0), txhi, txlo, whi, wlo)
            leave(pe, "tensor")
            enter(pe, "tensor", PH_H2, ("vector", "scalar"))
            agg_pe(pe, 1)
            leave(pe, "tensor")
            enter(pe, "tensor", PH_G2)
            pe.wait_ge(sem("w_lo"), KD * 3)
            gemm_pe(pe, 2, lambda t, u: vtin[:, u, :], slot_ready(1), vxhi, vxlo, wvhi, wvlo)
            leave(pe, "tensor")
            enter(pe, "tensor", PH_V)
            attention_pe(pe)
            leave(pe, "tensor")
            enter(pe, "tensor", PH_ATT)
            pe.wait_ge(sem("w_lo"), KD * 4)
            gemm_pe(pe, 3, lambda t, u: otin[:, u, :], slot_ready(2), oxhi, oxlo, wphi, wplo)
            leave(pe, "tensor")
            enter(pe, "tensor", PH_O)
            pe.sem_inc(sem("t2_raw"), 2)
            for t in range(T):
                pe.wait_ge(sem("t2_lo"), t + 1)
                for k in range(KD):
                    at = (t % 2 * 2 + k // 3) * BANK + k % 3 * P
                    last = pe.transpose(ps[:, at:at + P], xn2[:, t, k * 128:(k + 1) * 128], ident[0:P, 0:P])
                last.then_inc(sem("t2_raw"), 1)
            leave(pe, "tensor")
            enter(pe, "tensor", PH_T)
            pe.wait_ge(sem("wr_split"), 1)
            for c, (at, n) in enumerate(CHUNKS):
                for k in range(KD):
                    last = three(pe, bank(c, NE, n), wrhi[:, k, :], wrlo[:, k, :], yhi[:, k, at:at + n],
                                 ylo[:, k, at:at + n], k == 0, k == KD - 1)
                last.then_inc(sem("logt_raw"), 1)
            pe.wait_ge(sem("logt"), 3)
            for t in range(T):
                last = pe.transpose(ps[0:P, 3 * BANK + t * NE:3 * BANK + (t + 1) * NE], logt[:, t * P:(t + 1) * P], ident[0:NE, 0:NE])
            last.then_inc(sem("logit_raw"), 1)
            leave(pe, "tensor")
            enter(pe, "tensor", PH_R, ("vector", "scalar"))
            experts_pe(pe)

        @block.scalar
        def _(act):
            for t in range(T):
                act.wait_ge(sem(f"x_in{t // 5}"), 16)
                if t:
                    act.wait_ge(sem("ln_sum"), t)
                act.activation(esb[:, 0:D], xall[:, t, :], ACT.Copy, accum_out=lnc[:, t, 0:1]).then_inc(sem("ln_sum"), 1)
            for t in range(T):
                act.wait_ge(sem("ln_mean"), t + 1)
                act.activation(xall[:, t, :], xall[:, t, :], ACT.Identity, bias=lnc[:, t, 1:2]).then_inc(sem("ln_cen"), 1)
            act.wait_ge(sem("ln_cen"), T)
            for t in range(T):
                if t:
                    act.wait_ge(sem("ln_sq"), t)
                act.activation(esb[:, 0:D], xall[:, t, :], ACT.Square, accum_out=lnc[:, t, 2:3]).then_inc(sem("ln_sq"), 1)
            split_act(act, 0, wst, whi)
            act.wait_ge(sem("ln_var"), 1)
            act.activation(lnc[:, :, 4:5], lnc[:, :, 3:4], ACT.Sqrt).then_inc(sem("ln_sqrt"), 1)
            act.sem_inc(sem("block_read"), 2)
            with act.Fori(0, T // 2) as jj:
                for v in range(2):
                    act.wait_ge(sem("block_done"), 2 * jj + v + 1)
                    got = ps[0:P, 3 * v * BANK:3 * v * BANK + N]
                    act.activation(cnt[:, ds(2 * jj + v, 1), :].rearrange("p o n -> p (o n)"), got, ACT.Copy)
                    act.activation(far[:, ds(2 * jj + v, 1), :].rearrange("p o n -> p (o n)"), got, ACT.Relu,
                                   scale=-FAR, bias=viol[0:P, 2:3]).then_inc(sem("block_read"), 1)
            act.wait_ge(sem("ln_rstd"), 1)
            leave(act, "scalar")
            enter(act, "scalar", PH_EDGES, ("vector",))

            def normed(t, u):
                act.wait_ge(sem("tile_raw"), t + 1)
                act.activation(tin[:, u, :], xall[:, ds(t, 1), :].rearrange("p o d -> p (o d)"), ACT.Copy,
                               scale=lnc[:, ds(t, 1), 5:6].rearrange("p o c -> p (o c)")).then_inc(sem("h1_row"), 1)
            h_phase_act(act, 0, normed)
            leave(act, "scalar")
            enter(act, "scalar", PH_H1, ("tensor", "vector"))
            agg_act(act, 0, None)
            split_act(act, 1, wst, whi)
            leave(act, "scalar")
            enter(act, "scalar", PH_G1)
            h_phase_act(act, 1)
            leave(act, "scalar")
            enter(act, "scalar", PH_H2)

            def norms(t, u):
                act.wait_ge(sem("var_a"), t + 1)
                act.activation(stat[:, u, 1:2], stat[:, u, 1:2], ACT.Sqrt).then_inc(sem("root_a"), 1)
                act.wait_ge(sem("rstd_a"), t + 1)
                act.wait_ge(sem(f"xa_out{u}"), 8 * t + (16 - 8 * u))
                act.activation(xab[:, u, :], tin[:, u, :], ACT.Identity, scale=stat[:, u, 2:3], bias=stat[:, u, 3:4])\
                    .then_inc(sem("xa_row"), 1)
                act.wait_ge(sem("var_b"), t + 1)
                act.activation(stat[:, u, 5:6], stat[:, u, 5:6], ACT.Sqrt).then_inc(sem("root_b"), 1)
                act.wait_ge(sem("rstd_b"), t + 1)
                act.wait_ge(sem(f"xn_out{u}"), 8 * t + (16 - 8 * u))
                act.activation(xnb[:, u, :], xab[:, u, :], ACT.Identity, scale=stat[:, u, 6:7], bias=stat[:, u, 7:8])\
                    .then_inc(sem("xn_normed"), 1)
            agg_act(act, 1, norms)
            leave(act, "scalar")
            enter(act, "scalar", PH_G2)
            split_act(act, 2, wvst, wvhi)

            def v_hi(t, u):
                act.wait_ge(sem("v_copied"), t + 1)
                gemm_hi(act, 2, vxhi, t, u)

            def v_out(t, u):
                act.wait_ge(sem("tile_y"), t + (2 * T + 3))
                act.activation(val[:, ds(t, 1), :, 0:HD].rearrange("p o (a h) c -> p (o a) h c", a=2),
                               two(4 + 2 * u, P, HALF).rearrange("p a (h c) -> p a h c", c=HD), ACT.Copy)\
                    .then_inc(sem("tile_yfree"), 1)
            v_hi(0, 0)
            with act.Fori(0, T // 2 - 1) as i:
                v_hi(2 * i + 1, 1)
                v_out(2 * i, 0)
                v_hi(2 * i + 2, 0)
                v_out(2 * i + 1, 1)
            v_hi(T - 1, 1)
            v_out(T - 2, 0)
            v_out(T - 1, 1)
            leave(act, "scalar")
            enter(act, "scalar", PH_V)
            attention_act(act)
            leave(act, "scalar")
            enter(act, "scalar", PH_ATT)
            split_act(act, 3, wpst, wphi)

            def norm2(t, u):
                act.wait_ge(sem("var_c"), t + 1)
                act.activation(stat[:, u, 1:2], stat[:, u, 1:2], ACT.Sqrt).then_inc(sem("root_c"), 1)
                act.wait_ge(sem("rstd_c"), t + 1)
                act.activation(xn2[:, ds(t, 1), :].rearrange("p o d -> p (o d)"),
                               acc[:, ds(t, 1), :].rearrange("p o d -> p (o d)"), ACT.Identity,
                               scale=stat[:, u, 2:3], bias=stat[:, u, 3:4]).then_inc(sem("n2_normed"), 1)
            gemm_hi(act, 3, oxhi, 0, 0)
            with act.Fori(0, T // 2 - 1) as i:
                gemm_hi(act, 3, oxhi, 2 * i + 1, 1)
                norm2(2 * i, 0)
                gemm_hi(act, 3, oxhi, 2 * i + 2, 0)
                norm2(2 * i + 1, 1)
            gemm_hi(act, 3, oxhi, T - 1, 1)
            norm2(T - 2, 0)
            norm2(T - 1, 1)
            leave(act, "scalar")
            enter(act, "scalar", PH_O)
            with act.Fori(0, T // 2) as i:
                for u in range(2):
                    t = 2 * i + u
                    act.wait_ge(sem("t2_raw"), t + 3)
                    act.activation(yhi[:, :, ds(t * P, P)].rearrange("p (a k) c -> p a k c", a=2),
                                   two(2 * u, 128, 3 * P).rearrange("p a (k c) -> p a k c", c=P), ACT.Copy)\
                        .then_inc(sem("t2_hi"), 1)
            def split_w(n, e, st, hi):
                act.wait_ge(sem(f"{n}_in"), 16 * e + 16)
                act.activation(hi[:, :, :].rearrange("p k c -> p (k c)"), st[:, :, :].rearrange("p k c -> p (k c)"), ACT.Copy)\
                    .then_inc(sem(f"{n}_hi"), 1)
            split_w("w1", 0, w1st, w1hi)
            leave(act, "scalar")
            enter(act, "scalar", PH_T)
            act.wait_ge(sem("wr_in"), 16)
            act.activation(wrhi[:, :, :], wrst[:, :, :], ACT.Copy).then_inc(sem("wr_hi"), 1)
            for c, (at, n) in enumerate(CHUNKS):
                act.wait_ge(sem("logt_raw"), c + 1)
                act.activation(logt[:, at:at + n], bank(c, NE, n), ACT.Copy).then_inc(sem("logt"), 1)
            act.wait_ge(sem("gap"), 1)
            act.activation(gcol[:, :, 1:2], gcol[:, :, 0:1], ACT.Exp).then_inc(sem("gap_exp"), 1)
            leave(act, "scalar")
            enter(act, "scalar", PH_R, ("vector", "tensor"))
            act.sem_inc(sem("gelu"), 3)

            def expert(e, more):
                act.wait_ge(sem("hid"), 9 * e + 1)
                split_w("w2", e, w2st, w2hi)
                for j in range(KF * len(CHUNKS)):
                    c, f = j // KF, j % KF
                    n = CHUNKS[c][1]
                    act.wait_ge(sem("hid"), 9 * e + (j + 1))
                    act.wait_ge(sem("ht_free"), 9 * e + (j + 1))
                    act.activation(gel[:, j % 3, 0:n], bank(j % 3, 128, n), ACT.Gelu).then_inc(sem("gelu"), 1)
                if more:
                    split_w("w1", e + 1, w1st, w1hi)
            with act.Fori(0, NE - 1) as e:
                expert(e, True)
            expert(NE - 1, False)

        @block.vector
        def _(dve):
            order = Order(dve, sem("dve_order"))
            dve.sem_inc(sem("tile_lo"), 2)
            dve.sem_inc(sem("tile_yfree"), 2)
            dve.sem_inc(sem("agg_lo"), 1)
            dve.sem_inc(sem("agg_read"), 2)
            dve.sem_inc(sem("agg_maxed"), 1)
            dve.wait_ge(sem("consts"), 1)
            dve.wait_ge(sem("edges_in"), 96)
            dve.tensor_copy(efl[:, :, :, :], eraw[:, :, :, :]).then_inc(sem("edges_f"), 1)
            order.did(dve.memset(viol[:, 1:2], 1.0))
            order.did(dve.memset(viol[:, 2:3], FAR))
            dve.wait_ge(sem("edges_t"), 1)
            order.did(dve.tensor_copy(edge[:, :, LEAD:ECOLS], two(0, 128, 384)))
            order.wait()
            d_ = edge[:, 1, :]
            order.did(dve.tensor_tensor(lohi[:, 0, :], d_, lohi[:, 0, :], ALU.is_lt))
            order.did(dve.tensor_tensor(lohi[:, 1, :], d_, lohi[:, 1, :], ALU.is_ge))
            order.wait()
            order.did(dve.tensor_tensor(lohi[:, 0, :], lohi[:, 0, :], lohi[:, 1, :], ALU.add))
            order.wait()
            dve.scalar_tensor_tensor(lohi[:, 1, :], d_, 0.0, lohi[:, 0, :], ALU.is_ge, ALU.mult, accum_out=viol[:, 0:1])\
                .then_inc(sem("viol"), 1)
            dve.wait_ge(sem("viol_sum"), 1)
            dve.tensor_scalar(flag[0:1, 0:1], ps[0:1, 2 * BANK:2 * BANK + 1], 0.0, None, ALU.is_gt).then_inc(sem("flag"), 1)
            dve.wait_ge(sem("flag"), 1)
            spread = dve.value_load(flag[0:1, 0:1], min_val=0, max_val=1)

            def one_hots(steps, stride):
                turns = steps // 4
                with dve.Fori(0, T) as j:
                    def turn(r, first):
                        for u in range(4):
                            dve.wait_ge(sem("oh_free"), j * steps + r * 4 + (u + 1))
                            if first and u == 0:
                                s_col = d_col = selfc[:, ds(j, 1)]
                            else:
                                q = (j * stride + r * 4 + (u - 1)) if stride else (r * 4 + (u - 1))
                                s_col, d_col = edge[:, 0, ds(q, 1)], edge[:, 1, ds(q, 1)]
                            dve.tensor_scalar(ohd[:, u, :], iota[:, ds(j * P, P)], d_col, None, ALU.is_equal)
                            dve.tensor_scalar(ohs[:, u, :], iota[:, :], s_col, None, ALU.is_equal)\
                                .then_inc(sem("oh_ready"), 1)
                    turn(0, True)
                    with dve.Fori(1, turns) as r:
                        turn(r, False)
            with dve.If(spread == 0):
                one_hots(NEAR_STEPS, STRIDE)
            with dve.Else():
                one_hots(ALL_STEPS, 0)
            dve.wait_ge(sem("ln_sqrt"), 1)
            dve.reciprocal(lnc[:, :, 5:6], lnc[:, :, 4:5]).then_inc(sem("ln_rstd"), 1)
            leave(dve, "vector")
            dve.wait_ge(sem("att_in"), 32)
            h_phase_dve(dve, 0)
            diag_dve(dve, 0)
            leave(dve, "vector")
            enter(dve, "vector", PH_H1, ("tensor", "scalar"))
            dve.wait_ge(sem("brow_in"), 16)
            dve.wait_ge(sem("agg_esb"), 2)

            def finish1(t, u):
                dve.wait_ge(sem(f"g1_out{u}"), 8 * t + (16 - 8 * u))
                order.did(dve.scalar_tensor_tensor(halves(tin[:, u, :]), two(3 + 2 * u, P, HALF), zsum[:, u, 5:6],
                                                   halves(brow[:, :]), ALU.mult, ALU.add))
                order.wait()
                dve.sem_inc(sem("agg_read"), 1)
                dve.tensor_scalar(tin[:, u, :], tin[:, u, :], 0.0, None, ALU.max).then_inc(sem("g1_row"), 1)
            agg_dve(dve, order, 0, finish1, 1)
            leave(dve, "vector")
            enter(dve, "vector", PH_G1, ("scalar", "sync"))
            dve.wait_ge(sem("att_in"), 64)
            h_phase_dve(dve, 1)
            diag_dve(dve, 1)
            leave(dve, "vector")
            enter(dve, "vector", PH_H2, ("tensor", "scalar"))
            dve.wait_ge(sem("brow_in"), 32)
            dve.wait_ge(sem("agg_esb"), 4)

            def moments(row, u, c, v):
                for h in range(2):
                    order.did(dve.bn_stats(bn[:, u, 6 * h:6 * h + 6], row[:, h * HALF:(h + 1) * HALF]))
                order.wait()
                alone(dve)
                order.did(dve.bn_aggr(stat[:, u, c:c + 2], bn[:, u, :]))
                order.wait()
                dve.tensor_scalar(stat[:, u, c + 1:c + 2], stat[:, u, c + 1:c + 2], EPS, None, ALU.add).then_inc(sem(f"var_{v}"), 1)

            def inverse(t, u, c, v):
                dve.wait_ge(sem(f"root_{v}"), t + 1)
                order.did(dve.reciprocal(stat[:, u, c + 2:c + 3], stat[:, u, c + 1:c + 2]))
                order.wait()
                dve.scalar_tensor_tensor(stat[:, u, c + 3:c + 4], stat[:, u, c:c + 1], -1.0, stat[:, u, c + 2:c + 3],
                                         ALU.mult, ALU.mult).then_inc(sem(f"rstd_{v}"), 1)

            def finish2(t, u):
                dve.wait_ge(sem(f"x1_out{u}"), 8 * t + (16 - 8 * u))
                order.did(dve.scalar_tensor_tensor(halves(tin[:, u, :]), two(3 + 2 * u, P, HALF), zsum[:, u, 5:6],
                                                   halves(brow[:, :]), ALU.mult, ALU.add))
                order.wait()
                dve.sem_inc(sem("agg_read"), 1)
                dve.wait_ge(sem(f"xres_in{u}"), 8 * t + (16 - 8 * u))
                order.did(dve.tensor_tensor(tin[:, u, :], tin[:, u, :], xres[:, u, :], ALU.add))
                order.wait()
                dve.sem_inc(sem("xres_free"), 1)
                dve.sem_inc(sem("x1_row"), 1)
                moments(tin[:, u, :], u, 0, "a")
                inverse(t, u, 0, "a")
                dve.wait_ge(sem("xa_row"), t + 1)
                moments(xab[:, u, :], u, 4, "b")
                inverse(t, u, 4, "b")
            agg_dve(dve, order, 1, finish2, 2 + 2 * 4)
            leave(dve, "vector")
            enter(dve, "vector", PH_G2)
            with dve.Fori(0, T // 2) as i:
                gemm_lo(dve, 2, vxhi, vxlo, 2 * i, 0)
                gemm_lo(dve, 2, vxhi, vxlo, 2 * i + 1, 1)
            leave(dve, "vector")
            enter(dve, "vector", PH_V)
            attention_dve(dve, order)
            leave(dve, "vector")
            enter(dve, "vector", PH_ATT)
            dve.sem_inc(sem("xar_free"), 2)

            def residual(t, u):
                row = acc[:, ds(t, 1), :].rearrange("p o d -> p (o d)")
                dve.wait_ge(sem("tile_y"), t + (3 * T + 3))
                dve.wait_ge(sem(f"xar_in{u}"), 8 * t + (16 - 8 * u))
                order.did(dve.tensor_tensor(halves(row), two(4 + 2 * u, P, HALF), halves(xain[:, u, :]), ALU.add))
                order.wait()
                dve.sem_inc(sem("xar_free"), 1)
                dve.sem_inc(sem("tile_yfree"), 1)
                moments(row, u, 0, "c")
                inverse(t, u, 0, "c")
            gemm_lo(dve, 3, oxhi, oxlo, 0, 0)
            with dve.Fori(0, T // 2 - 1) as i:
                order.loop(i, 2 * 5)
                gemm_lo(dve, 3, oxhi, oxlo, 2 * i + 1, 1)
                residual(2 * i, 0)
                gemm_lo(dve, 3, oxhi, oxlo, 2 * i + 2, 0)
                residual(2 * i + 1, 1)
            order.end(T // 2 - 1)
            gemm_lo(dve, 3, oxhi, oxlo, T - 1, 1)
            residual(T - 2, 0)
            residual(T - 1, 1)
            leave(dve, "vector")
            enter(dve, "vector", PH_O)
            dve.sem_inc(sem("t2_lo"), 2)
            with dve.Fori(0, T // 2) as i:
                for u in range(2):
                    t = 2 * i + u
                    dve.wait_ge(sem("t2_hi"), t + 1)
                    dve.tensor_tensor(ylo[:, :, ds(t * P, P)].rearrange("p (a k) c -> p a k c", a=2),
                                      two(2 * u, 128, 3 * P).rearrange("p a (k c) -> p a k c", c=P),
                                      yhi[:, :, ds(t * P, P)].rearrange("p (a k) c -> p a k c", a=2).bitcast(f32),
                                      ALU.subtract).then_inc(sem("t2_lo"), 1)
            leave(dve, "vector")
            enter(dve, "vector", PH_T)
            dve.wait_ge(sem("wr_hi"), 1)
            dve.tensor_tensor(wrlo[:, :, :], wrst[:, :, :], wrhi[:, :, :].bitcast(f32), ALU.subtract).then_inc(sem("wr_split"), 1)
            dve.wait_ge(sem("logit_raw"), 1)
            order.did(dve.tensor_copy(logit[:, :, :].rearrange("p t e -> p (t e)"), ps[0:P, 3 * BANK:3 * BANK + T * NE]))
            order.wait()
            for t in range(T):
                order.did(dve.max(top8[:, t, :], logit[:, t, :]))
            order.wait()
            for t in range(T):
                order.did(dve.max_index(ix8[:, t, :], top8[:, t, :], logit[:, t, :]))
            order.wait()
            order.did(dve.tensor_copy(ixf[:, :, :], ix8[:, :, 0:2]))
            order.did(dve.tensor_tensor(gcol[:, :, 0:1], top8[:, :, 1:2], top8[:, :, 0:1], ALU.subtract))
            order.wait()
            dve.sem_inc(sem("gap"), 1)
            dve.wait_ge(sem("gap_exp"), 1)
            order.did(dve.tensor_scalar(gcol[:, :, 0:1], gcol[:, :, 1:2], 1.0, None, ALU.add))
            order.wait()
            order.did(dve.reciprocal(gcol[:, :, 2:3], gcol[:, :, 0:1]))
            order.wait()
            order.did(dve.tensor_tensor(gcol[:, :, 3:4], gcol[:, :, 1:2], gcol[:, :, 2:3], ALU.mult))
            dve.wait_ge(sem("iota8"), 1)
            for w in range(2):
                order.did(dve.tensor_tensor(hot[:, w, :, :], iota8[:, :].rearrange("p (o e) -> p o e", o=1).broadcast_to([P, T, NE]),
                                            ixf[:, :, w:w + 1].broadcast_to([P, T, NE]), ALU.is_equal))
            order.wait()
            for w in range(2):
                order.did(dve.tensor_tensor(hot[:, w, :, :], hot[:, w, :, :],
                                            gcol[:, :, 2 + w:3 + w].broadcast_to([P, T, NE]), ALU.mult))
            order.wait()
            order.did(dve.tensor_tensor(gate[:, :, :], hot[:, 0, :, :], hot[:, 1, :, :], ALU.add))
            order.wait()
            leave(dve, "vector")
            enter(dve, "vector", PH_R, ("scalar", "tensor"))
            dve.sem_inc(sem("ht_free"), 3)
            dve.sem_inc(sem("added"), 2)

            def expert(e, last):
                for j in range(KF * len(CHUNKS)):
                    c, f = j // KF, j % KF
                    at, n = CHUNKS[c]
                    dve.wait_ge(sem("gelu"), 9 * e + (j + 4))
                    dve.tensor_copy(hthi[:, f, at:at + n], gel[:, j % 3, 0:n]).then_inc(sem("ht_hi"), 1)
                    dve.wait_ge(sem("ht_hi"), 9 * e + (j + 1))
                    dve.tensor_tensor(htlo[:, f, at:at + n], gel[:, j % 3, 0:n], hthi[:, f, at:at + n].bitcast(f32), ALU.subtract)\
                        .then_inc(sem("ht"), 1)
                    dve.wait_ge(sem("ht"), 9 * e + (j + 1))
                    dve.sem_inc(sem("ht_free"), 1)
                for t in range(T):
                    dve.wait_ge(sem("ey"), T * e + (t + 1))
                    dve.scalar_tensor_tensor(halves(acc[:, t, :]), two(3 + 2 * (t % 2), P, HALF), gate[:, t, ds(e, 1)],
                                             halves(acc[:, t, :]), ALU.mult, ALU.add).then_inc(sem("added"), 1)
                    if last:
                        dve.wait_ge(sem("added"), T * e + (t + 3))
                        dve.sem_inc(sem("final"), 1)
            with dve.Fori(0, NE - 1) as e:
                expert(e, False)
            expert(NE - 1, True)


_INS = ['x', 'src', 'dst', 'L0_gnn_W1', 'L0_gnn_att_src1', 'L0_gnn_att_dst1', 'L0_gnn_b1', 'L0_gnn_W2',
        'L0_gnn_att_src2', 'L0_gnn_att_dst2', 'L0_gnn_b2', 'L0_ffn_Wqkv', 'L0_ffn_Wproj', 'L0_ffn_Wrouter',
        'L0_ffn_W1', 'L0_ffn_W2', 'L0_ffn_ln1_g', 'L0_ffn_ln1_b', 'L0_ffn_ln2_g', 'L0_ffn_ln2_b']


def kernel(**inputs):
    import concourse.bacc as _bacc
    from concourse.bass_utils import run_bass_kernel_spmd as _run

    nc = _bacc.Bacc("TRN2", target_bir_lowering=False, num_devices=1)
    arrays, args = {}, []
    for name in _INS:
        a = np.ascontiguousarray(inputs[name])
        arrays[f"in_{name}_dram"] = a
        args.append(nc.dram_tensor(f"in_{name}_dram", a.shape, mybir.dt.from_np(a.dtype), kind="ExternalInput").ap())
    o = nc.dram_tensor("out_0_dram", (N, D), mybir.dt.float32, kind="ExternalOutput").ap()
    build(nc, *args, o)
    r = _run(nc, [arrays], core_ids=[0])
    return r.results[0]["out_0_dram"]
```

```python
import numpy as np
import concourse.bass as bass
from concourse import mybir
from contextlib import ExitStack

N = 1250
P = 125
T = N // P
D = 768
KD = D // 128
HALF = D // 2
EDGES = 41250
H = 12
HD = D // H
NE = 8
FF = 384
KF = FF // 128
EPS = 1e-5
SLOPE = 0.2
FAR = 1e30
CHUNKS = [(0, 418), (418, 416), (834, 416)]
GQ = 250
NG = N // GQ
UNITS = NG * T // 2
RING = 5
LAG = 3
BANK = 512

EROWS = -(-EDGES // 128)
LEAD = 3
ECOLS = LEAD + 3 * 128
ALL_STEPS = 1 + LEAD + EROWS + (-(1 + LEAD + EROWS)) % 8
STRIDE = 32
NEAR_STEPS = 40
WINDOW = NEAR_STEPS - 1


class Order:

    def __init__(self, eng, sem):
        self.eng, self.sem, self.base, self.turn, self.n = eng, sem, 0, 0, 0

    def did(self, ins):
        ins.then_inc(self.sem, 1)
        self.n += 1

    def wait(self):
        self.eng.wait_ge(self.sem, self.turn + (self.base + self.n))

    def loop(self, i, per):
        self.base, self.n, self.turn, self.per = self.base + self.n, 0, i * per, per

    def end(self, turns):
        assert self.n == self.per, (self.n, self.per)
        self.base, self.n, self.turn = self.base + turns * self.per, 0, 0


def build(nc, x, src, dst, gw1, gas1, gad1, gb1, gw2, gas2, gad2, gb2,
          wqkv, wproj, wrouter, w1, w2, ln1g, ln1b, ln2g, ln2b, out):
    f32, f32r, bf16, f16 = mybir.dt.float32, mybir.dt.float32r, mybir.dt.bfloat16, mybir.dt.float16
    i32, u32, u16 = mybir.dt.int32, mybir.dt.uint32, mybir.dt.uint16
    ALU, ACT, AX = mybir.AluOpType, mybir.ActivationFunctionType, mybir.AxisListType
    size = {f32: 4, f32r: 4, bf16: 2, f16: 2, i32: 4, u32: 4, u16: 2}
    ds = bass.ds

    hid_d = nc.dram_tensor("hid_d", (N, D), f32).ap()
    x1_d = nc.dram_tensor("x1_d", (N, D), f32).ap()
    xa_d = nc.dram_tensor("xa_d", (N, D), f32).ap()
    xn_d = nc.dram_tensor("xn_d", (N, D), f32).ap()

    base = (nc.sbuf_base + 63) // 64 * 64
    top = [0]

    def put(name, shape, dt, at=None):
        n = int(np.prod(shape[1:])) * size[dt]
        n = (n + 31) // 32 * 32
        if at is None:
            at = top[0]
            top[0] += n
        put.end = at + n
        assert base + put.end <= nc.sbuf_usable_end, (name, put.end)
        return nc.alloc_sbuf_tensor_at(name, shape, dt, offset=base + at)

    ident = put("ident", [128, 128], f32)
    ones = put("ones", [P, P], f32)
    flag = put("flag", [1, 2], i32)
    bn = put("bn", [P, 2, 12], f32)
    stat = put("stat", [P, 2, 8], f32)
    es = put("es", [P, T], f32)
    ed = put("ed", [P, T], f32)
    ed02 = put("ed02", [P, T], f32)
    zsum = put("zsum", [P, 2, 8], f32)
    wsum = put("wsum", [P, T], f32)
    lnc = put("lnc", [P, T, 6], f32)
    mcol = put("mcol", [P, 2, T], f32)
    gate = put("gate", [P, T, NE], f32)
    FREE = top[0]

    att = put("att", [P, 2, D], f32)
    brow = put("brow", [P, D], f32)
    WAT = top[0]
    whi = put("whi", [128, KD, D], f32r)
    wlo = put("wlo", [128, KD, D], f32r)
    hhi = put("hhi", [P, T, D], f32r)
    HLO = top[0]
    hlo = put("hlo", [P, T, D], f32r)
    xall = put("xall", [P, T, D], f32, at=HLO)
    cnt = put("cnt", [P, T, N], u16)
    far = put("far", [P, T, N], bf16)
    esb = put("esb", [P, N], f32)
    LAT = top[0]
    lg2 = put("lg2", [P, 2, N], f32)
    cand = put("cand", [P, N], bf16)
    tin = put("tin", [P, 2, D], f32)
    wst = put("wst", [128, 2, D], f32)
    PTAT = top[0]
    pthi = put("pthi", [P, 2, N], f32r)
    ptlo = put("ptlo", [P, 2, N], f32r)
    txhi = put("txhi", [128, 2, D - 18], f32r, at=PTAT)
    txlo = put("txlo", [128, 2, D - 18], f32r, at=put.end)
    xres = put("xres", [P, 2, D], f32, at=WAT)
    xab = put("xab", [P, 2, D], f32, at=put.end)
    xnb = put("xnb", [P, 2, D], f32, at=put.end)
    lnrow = put("lnrow", [P, 2, D], f32, at=put.end)
    ohs = put("ohs", [128, 4, N], f16, at=LAT)
    ohd = put("ohd", [128, 4, P], f16, at=PTAT)
    iota = put("iota", [128, N], f16, at=put.end)
    edge = put("edge", [128, 2, ECOLS], f32, at=put.end)
    selfc = put("selfc", [128, T], f32, at=put.end)
    eraw = put("eraw", [128, 2, 3, 128], i32, at=put.end)
    efl = put("efl", [128, 2, 3, 128], f32, at=put.end)
    lohi = put("lohi", [128, 2, ECOLS], f32, at=put.end)
    viol = put("viol", [128, 4], f32, at=put.end)
    GRAPH_TOP = top[0]

    XT = FREE
    xthi = put("xthi", [128, KD, N], f32r, at=XT)
    xtlo = put("xtlo", [128, KD, N], f32r, at=put.end)
    VAT = put.end
    val = put("val", [P, H // 2, T, 128], f32, at=VAT)
    HEADS = put.end
    outt = put("outt", [128, H // 2, T * 128], f32, at=VAT)
    qst = put("qst", [128, 2, N], f32r, at=HEADS)
    q2 = put("q2", [128, 2, N], f32r, at=put.end)
    kst = put("kst", [128, 2, N], f32r, at=put.end)
    k2 = put("k2", [128, 2, N], f32r, at=put.end)
    raw = put("raw", [128, 2, N], f32, at=put.end)
    wqhi = put("wqhi", [128, 2, KD, 128], f32r, at=put.end)
    wqlo = put("wqlo", [128, 2, KD, 128], f32r, at=put.end)
    wqst = put("wqst", [128, 2, KD, 128], f32, at=put.end)
    prob = put("prob", [P, 3, 2 * GQ], f32, at=put.end)
    prhi = put("prhi", [P, RING, 2 * GQ], f32r, at=put.end)
    prlo = put("prlo", [P, RING, 2 * GQ], f32r, at=put.end)
    vhi = put("vhi", [P, 2, T, 128], f32r, at=put.end)
    vlo = put("vlo", [P, 2, T, HD], f32r, at=put.end)
    rz = put("rz", [HD, 2, GQ], f32, at=put.end)
    wvhi = put("wvhi", [128, KD, D], f32r, at=HEADS)
    wvlo = put("wvlo", [128, KD, D], f32r, at=put.end)
    wvst = put("wvst", [128, KD, D], f32, at=put.end)
    vtin = put("vtin", [P, 2, D], f32, at=put.end)
    vxhi = put("vxhi", [128, 2, D - 18], f32r, at=put.end)
    vxlo = put("vxlo", [128, 2, D - 18], f32r, at=put.end)
    wphi = put("wphi", [128, KD, D], f32r, at=XT)
    wplo = put("wplo", [128, KD, D], f32r, at=put.end)
    oxhi = put("oxhi", [128, 2, D - 18], f32r, at=put.end)
    oxlo = put("oxlo", [128, 2, D - 18], f32r, at=put.end)
    wpst = put("wpst", [128, 2, D], f32, at=put.end)
    assert put.end <= VAT
    yhi = put("yhi", [128, KD, N], f32r, at=VAT)
    acc = put("acc", [P, T, D], f32, at=HEADS)
    XT2 = put.end
    ylo = put("ylo", [128, KD, N], f32r, at=XT2)
    XN2 = put.end
    xn2 = put("xn2", [P, T, D], f32, at=XN2)
    row2 = put("row2", [P, 2, D], f32, at=put.end)
    xain = put("xain", [P, 2, D], f32, at=put.end)
    x1in = put("x1in", [P, 2, D], f32, at=XT2)
    w1hi = put("w1hi", [128, KD, FF], f32r, at=XT)
    w1lo = put("w1lo", [128, KD, FF], f32r, at=put.end)
    w2hi = put("w2hi", [128, KF, D], f32r, at=put.end)
    w2lo = put("w2lo", [128, KF, D], f32r, at=put.end)
    w1st = put("w1st", [128, KD, FF], f32, at=put.end)
    w2st = put("w2st", [128, KF, D], f32, at=put.end)
    assert put.end <= VAT
    hthi = put("hthi", [128, KF, N], f32r, at=XN2)
    htlo = put("htlo", [128, KF, N], f32r, at=put.end)
    gel = put("gel", [128, 3, CHUNKS[0][1]], f32, at=put.end)
    wrhi = put("wrhi", [128, KD, NE], f32r, at=put.end)
    wrlo = put("wrlo", [128, KD, NE], f32r, at=put.end)
    wrst = put("wrst", [128, KD, NE], f32, at=put.end)
    logt = put("logt", [NE, N], f32, at=put.end)
    logit = put("logit", [P, T, NE], f32, at=put.end)
    top8 = put("top8", [P, T, 8], f32, at=put.end)
    ix8 = put("ix8", [P, T, 8], u32, at=put.end)
    ixf = put("ixf", [P, T, 2], f32, at=put.end)
    iota8 = put("iota8", [P, NE], f32, at=put.end)
    hot = put("hot", [P, 2, T, NE], f32, at=put.end)
    gcol = put("gcol", [P, T, 4], f32, at=put.end)

    ctx = ExitStack()
    with ctx:
        ps = ctx.enter_context(nc.psum_tensor("ps", [128, 8 * BANK], f32))
        sems = {}

        def sem(name):
            if name not in sems:
                sems[name] = ctx.enter_context(nc.semaphore(name))
            return sems[name]

        def bank(b, rows=128, cols=BANK):
            return ps[0:rows, b * BANK:b * BANK + cols]

        def two(b, rows, cols):
            return ps[0:rows, b * BANK:(b + 2) * BANK].rearrange("p (a c) -> p a c", a=2)[:, :, 0:cols]

        def halves(ap):
            return ap.rearrange("p (a c) -> p a c", a=2)

        ENGINES = ("tensor", "vector", "scalar", "gpsimd", "sync")

        def alone(eng):
            eng.sem_inc(sem("passed"), 1)

        def leave(eng, name):
            eng.drain().then_inc(sem(f"left_{name}"), 1)

        def enter(eng, name, phase, others=ENGINES):
            for o in others:
                if o != name:
                    eng.wait_ge(sem(f"left_{o}"), phase)

        def three(pe, o, lhi, llo, rhi, rlo, start, stop):
            pe.matmul(o, lhi, rhi, start=start, stop=False)
            pe.matmul(o, llo, rhi, start=False, stop=False)
            return pe.matmul(o, lhi, rlo, start=False, stop=stop)

        def load_split_sp(sp, n, dram, stage):
            for k in range(KD):
                if k >= 2:
                    sp.wait_ge(sem("w_lo"), KD * n + k - 1)
                sp.dma_start(stage[:, k % 2, :], dram[k * 128:(k + 1) * 128, :]).then_inc(sem(f"w_in{k % 2}"), 16)

        def split_act(act, n, stage, hi, chunks=range(KD)):
            for k in chunks:
                act.wait_ge(sem(f"w_in{k % 2}"), 16 * (KD // 2 * n + k // 2 + 1))
                act.activation(hi[:, k, :], stage[:, k % 2, :], ACT.Copy).then_inc(sem("w_hi"), 1)

        def split_pool(pool, n, stage, hi, lo, chunks=range(KD)):
            for k in chunks:
                pool.wait_ge(sem("w_hi"), KD * n + k + 1)
                pool.tensor_tensor(lo[:, k, :], stage[:, k % 2, :], hi[:, k, :].bitcast(f32), ALU.subtract)\
                    .then_inc(sem("w_lo"), 1)

        def gemm_pe(pe, n, source, ready, hi, lo, whi_, wlo_):

            def transposes(t, u):
                if source is None:
                    return
                ready(t, u)
                pe.wait_ge(sem("tile_lo"), t + (T * n + 1))
                tile = source(t, u)
                for k in range(KD):
                    last = pe.transpose(ps[:, (2 * u + k // 3) * BANK + k % 3 * P:(2 * u + k // 3) * BANK + (k % 3 + 1) * P],
                                        tile[:, k * 128:(k + 1) * 128], ident[0:P, 0:P])
                last.then_inc(sem("tile_raw"), 1)

            def product(t, u):
                pe.wait_ge(sem("tile_lo"), t + (T * n + 3))
                pe.wait_ge(sem("tile_yfree"), t + (T * n + 1))
                for h in range(2):
                    for k in range(KD):
                        last = three(pe, bank(4 + 2 * u + h, P, HALF), hi[:, u, k * P:(k + 1) * P],
                                     lo[:, u, k * P:(k + 1) * P], whi_[:, k, h * HALF:(h + 1) * HALF],
                                     wlo_[:, k, h * HALF:(h + 1) * HALF], k == 0, k == KD - 1)
                last.then_inc(sem("tile_y"), 1)

            transposes(0, 0)
            with pe.Fori(0, T // 2 - 1) as i:
                transposes(2 * i + 1, 1)
                product(2 * i, 0)
                transposes(2 * i + 2, 0)
                product(2 * i + 1, 1)
            transposes(T - 1, 1)
            product(T - 2, 0)
            product(T - 1, 1)

        def gemm_hi(act, n, hi, t, u):
            act.wait_ge(sem("tile_raw"), t + (T * n + 3))
            act.wait_ge(sem("tile_y"), t + (T * n + 1))
            act.activation(halves(hi[:, u, :]), two(2 * u, 128, 3 * P), ACT.Copy).then_inc(sem("tile_hi"), 1)

        def gemm_lo(dve, n, hi, lo, t, u):
            dve.wait_ge(sem("tile_hi"), t + (T * n + 1))
            dve.tensor_tensor(halves(lo[:, u, :]), two(2 * u, 128, 3 * P), halves(hi[:, u, :]).bitcast(f32),
                              ALU.subtract).then_inc(sem("tile_lo"), 1)

        def ring_sp(sp, n, dram, ring, start=0, end=T // 2):
            with sp.Fori(start, end) as i:
                for u in range(2):
                    sp.wait_ge(sem("tile_raw"), 2 * i + (T * n + u + 1))
                    sp.dma_start(ring[:, u, :], dram.rearrange("(t p) d -> p t d", p=P)[:, ds(2 * i + u, 1), :])\
                        .then_inc(sem(f"tile_in{u}"), 16)

        def scores_dve(dve, n, i, u):
            t = 2 * i + u
            y = two(4 + 2 * u, P, HALF)
            dve.wait_ge(sem("tile_y"), t + (T * n + 3))
            dve.wait_ge(sem("tile_yhi"), t + (T * n + 1))
            dve.wait_ge(sem("tile_yfree"), t + (T * n + 2))
            for a, col in ((0, es), (1, ed)):
                dve.scalar_tensor_tensor(halves(lg2[:, a, 0:D]), y, 1.0, halves(att[:, a, :]), ALU.mult, ALU.mult,
                                         accum_out=col[:, ds(t, 1)])
            dve.tensor_tensor(halves(hlo[:, ds(t, 1), :].rearrange("p o d -> p (o d)")), y,
                              halves(hhi[:, ds(t, 1), :].rearrange("p o d -> p (o d)")).bitcast(f32), ALU.subtract)\
                .then_inc(sem("tile_yfree"), 1)

        def scores_act(act, n, i, u):
            t = 2 * i + u
            act.wait_ge(sem("tile_y"), t + (T * n + 3))
            act.activation(halves(hhi[:, ds(t, 1), :].rearrange("p o d -> p (o d)")), two(4 + 2 * u, P, HALF), ACT.Copy)\
                .then_inc(sem("tile_yhi"), 1)

        def h_phase_dve(dve, n):
            gemm_lo(dve, n, txhi, txlo, 0, 0)
            with dve.Fori(0, T // 2 - 1) as i:
                gemm_lo(dve, n, txhi, txlo, 2 * i + 1, 1)
                scores_dve(dve, n, i, 0)
                gemm_lo(dve, n, txhi, txlo, 2 * i + 2, 0)
                scores_dve(dve, n, i, 1)
            gemm_lo(dve, n, txhi, txlo, T - 1, 1)
            scores_dve(dve, n, T // 2 - 1, 0)
            scores_dve(dve, n, T // 2 - 1, 1)

        def h_phase_act(act, n, row=None):
            row = row or (lambda t, u: None)
            row(0, 0)
            row(1, 1)
            gemm_hi(act, n, txhi, 0, 0)
            with act.Fori(0, T // 2 - 1) as i:
                gemm_hi(act, n, txhi, 2 * i + 1, 1)
                row(2 * i + 2, 0)
                scores_act(act, n, i, 0)
                gemm_hi(act, n, txhi, 2 * i + 2, 0)
                row(2 * i + 3, 1)
                scores_act(act, n, i, 1)
            gemm_hi(act, n, txhi, T - 1, 1)
            scores_act(act, n, T // 2 - 1, 0)
            scores_act(act, n, T // 2 - 1, 1)

        def diag_dve(dve, n):
            dve.wait_ge(sem("tile_yfree"), T * (n + 1) + 2)
            dve.tensor_scalar(ed02[:, :], ed[:, :], SLOPE, None, ALU.mult)
            dve.tensor_tensor(lg2[:, 0, :].rearrange("p (t c) -> p t c", t=T),
                              ident[0:P, 0:P].rearrange("p (o c) -> p o c", o=1).broadcast_to([P, T, P]),
                              es[:, :].rearrange("p (t o) -> p t o", o=1).broadcast_to([P, T, P]), ALU.mult)\
                .then_inc(sem("agg_diag"), 1)

        def agg_pe(pe, n):
            pe.wait_ge(sem("agg_diag"), n + 1)
            for b, c in ((0, 500), (1, 500), (2, 250)):
                last = pe.matmul(bank(b, P, c), ones[:, :], lg2[:, 0, 500 * b:500 * b + c], start=True, stop=True)
            last.then_inc(sem("agg_esb_raw"), 1)

            def transposes(t, u):
                pe.wait_ge(sem("agg_w"), t + (T * n + 1))
                pe.wait_ge(sem("agg_lo"), t + (T * n + 1))
                for s in range(T):
                    at = (s // 4) * BANK + s % 4 * P
                    last = pe.transpose(ps[0:P, at:at + P], lg2[:, u, s * P:(s + 1) * P], ident[0:P, 0:P])
                last.then_inc(sem("agg_raw"), 1)

            def sums(t, u):
                pe.wait_ge(sem("agg_lo"), t + (T * n + 2))
                pe.wait_ge(sem("agg_read"), t + (T * n + 1))
                for h in range(2):
                    for s in range(T):
                        last = three(pe, bank(3 + 2 * u + h, P, HALF), pthi[:, u, s * P:(s + 1) * P],
                                     ptlo[:, u, s * P:(s + 1) * P], hhi[:, s, h * HALF:(h + 1) * HALF],
                                     hlo[:, s, h * HALF:(h + 1) * HALF], s == 0, s == T - 1)
                last.then_inc(sem("agg_sum"), 1)

            transposes(0, 0)
            with pe.Fori(0, T // 2 - 1) as i:
                transposes(2 * i + 1, 1)
                sums(2 * i, 0)
                transposes(2 * i + 2, 0)
                sums(2 * i + 1, 1)
            transposes(T - 1, 1)
            sums(T - 2, 0)
            sums(T - 1, 1)

        def agg_pool(pool, n, extra=None, early=None):
            pool.wait_ge(sem("agg_esb"), 2 * n + 2)

            def candidates(t):
                pool.wait_ge(sem("agg_maxed"), t + (T * n + 1))
                alone(pool)
                pool.tensor_tensor(cand[:, :], esb[:, :], far[:, ds(t, 1), :].rearrange("p o n -> p (o n)"),
                                   ALU.subtract).then_inc(sem("agg_cand"), 1)

            if early:
                for k in range(3):
                    candidates(k)
                for k in range(3):
                    early(k)
                    candidates(3 + k)
            else:
                with pool.Fori(0, T - 4) as t:
                    candidates(t)
            for k in range(4):
                candidates(T - 4 + k)
                if extra:
                    extra(k, k % 2)
            if extra:
                with pool.Fori(0, (T - 4) // 2) as i:
                    for v in range(2):
                        extra(2 * i + (4 + v), v)

        def agg_steps(eng, step, order=None, per=0):
            for k in range(3):
                step(k, k)
            with eng.Fori(0, (T - 6) // 2) as i:
                if order:
                    order.loop(i, 2 * per)
                for k in (3, 4):
                    step(2 * i + k, k)
            if order:
                order.end((T - 6) // 2)
            for k in range(T - 3, T + 3):
                step(k, k)

        def agg_act(act, n, extra=None):
            act.wait_ge(sem("agg_esb_raw"), n + 1)
            act.activation(halves(esb[:, 0:1000]), two(0, P, 500), ACT.Copy).then_inc(sem("agg_esb"), 1)
            act.activation(esb[:, 1000:N], bank(2, P, 250), ACT.Copy).then_inc(sem("agg_esb"), 1)
            act.wait_ge(sem("agg_esb"), 2 * n + 2)

            def sloped(t, u):
                act.wait_ge(sem("agg_raw"), t + (T * n + 1))
                act.activation(lg2[:, u, :], esb[:, :], ACT.Identity, scale=SLOPE, bias=ed02[:, ds(t, 1)])\
                    .then_inc(sem("agg_sl"), 1)

            def exponential(t, u):
                act.wait_ge(sem("agg_l"), t + (T * n + 1))
                act.activation(lg2[:, u, :], lg2[:, u, :], ACT.Exp, bias=zsum[:, u, 0:1]).then_inc(sem("agg_e"), 1)

            def higher(t, u):
                act.wait_ge(sem("agg_raw"), t + (T * n + 3))
                act.wait_ge(sem("agg_sum"), t + (T * n + 1))
                act.activation(halves(pthi[:, u, 0:1000]), two(0, P, 500), ACT.Copy).then_inc(sem("agg_hi"), 1)
                act.activation(pthi[:, u, 1000:N], bank(2, P, 250), ACT.Copy).then_inc(sem("agg_hi"), 1)

            def step(s, k):
                u = k % 2
                if k + 1 < T:
                    exponential(s + 1, 1 - u)
                if k < T:
                    higher(s, u)
                if k + 2 < T:
                    sloped(s + 2, u)
                if extra:
                    extra(s, k)

            sloped(0, 0)
            sloped(1, 1)
            exponential(0, 0)
            agg_steps(act, step)

        def agg_dve(dve, order, n, per, before, finish, after):
            def maximum(t, u):
                dve.wait_ge(sem("agg_cand"), t + (T * n + 1))
                order.did(dve.tensor_reduce(zsum[:, u, 2:3], cand[:, :], AX.X, ALU.max))
                order.wait()
                dve.sem_inc(sem("agg_maxed"), 1)
                order.did(dve.tensor_scalar(zsum[:, u, 3:4], zsum[:, u, 2:3], ed[:, ds(t, 1)], -1.0, ALU.add, ALU.mult))
                order.wait()
                dve.scalar_tensor_tensor(zsum[:, u, 0:1], zsum[:, u, 3:4], SLOPE, zsum[:, u, 3:4], ALU.mult, ALU.min)\
                    .then_inc(sem("agg_m"), 1)

            def leaky(t, u):
                dve.wait_ge(sem("agg_sl"), t + (T * n + 1))
                dve.wait_ge(sem("agg_m"), t + (T * n + 1))
                dve.scalar_tensor_tensor(lg2[:, u, :], esb[:, :], ed[:, ds(t, 1)], lg2[:, u, :], ALU.add, ALU.max)\
                    .then_inc(sem("agg_l"), 1)

            def weigh(t, u):
                dve.wait_ge(sem("agg_e"), t + (T * n + 1))
                dve.scalar_tensor_tensor(lg2[:, u, :], lg2[:, u, :], 1.0,
                                         cnt[:, ds(t, 1), :].rearrange("p o n -> p (o n)"), ALU.mult, ALU.mult,
                                         accum_out=wsum[:, ds(t, 1)]).then_inc(sem("agg_w"), 1)

            def lower(t, u):
                dve.wait_ge(sem("agg_hi"), 2 * t + (2 * T * n + 2))
                dve.tensor_tensor(halves(ptlo[:, u, 0:1000]), two(0, P, 500), halves(pthi[:, u, 0:1000]).bitcast(f32), ALU.subtract)
                dve.tensor_tensor(ptlo[:, u, 1000:N], bank(2, P, 250), pthi[:, u, 1000:N].bitcast(f32), ALU.subtract)\
                    .then_inc(sem("agg_lo"), 1)

            def ending(t, u):
                order.did(dve.reciprocal(zsum[:, u, 5:6], wsum[:, ds(t, 1)]))
                dve.wait_ge(sem("agg_sum"), t + (T * n + 3))
                order.wait()
                finish(t, u)

            def step(s, k):
                u = k % 2
                if k + 1 < T:
                    weigh(s + 1, 1 - u)
                if k < T:
                    lower(s, u)
                before(s, k)
                if 0 <= k - 2 < T:
                    ending(s - 2, u)
                if k + 2 < T:
                    leaky(s + 2, u)
                after(s, k)
                if k + 3 < T:
                    maximum(s + 3, 1 - u)

            maximum(0, 0)
            leaky(0, 0)
            maximum(1, 1)
            leaky(1, 1)
            weigh(0, 0)
            maximum(2, 0)
            dve.wait_ge(sem("agg_w"), T * n + 1)
            agg_steps(dve, step, order, per)
            dve.wait_ge(sem("agg_w"), T * (n + 1))

        PV0 = UNITS + RING
        PAIR = 2 * UNITS
        ROUGH_AT = ((5, 7, 9, 11, 13, 15, 17, 19, 21, 23), (6, 8, 10, 12, 14, 16, 17, 19, 21, 22))
        OUT_AT = ((9, 13, 19, 23), (8, 14, 19, 23))
        MAXIMA_AT = (24, 23)
        SET_M_AT = (24, 23)
        SPLIT_AT, SET_K_AT, SET_Q_AT, SPLIT_QK_AT = (1, 2), 3, 7, 9

        def place(e, j):
            n = UNITS * e + j
            return n % 3, 2 if n < 2 else 3

        def by_pool(j):
            return j % 5 in (0, 2, 4)

        def wait_lo(eng, p, e, j):
            n = UNITS * e + j
            pool = by_pool(j)
            each = sum(by_pool(k) == pool for k in range(PAIR))
            count = sum(by_pool(k) == pool for k in range(n + 1)) - sum(by_pool(k) == pool for k in range(n + 1, 0))
            eng.wait_ge(sem("pr_lo_pool" if pool else "pr_lo"), each * p + (count + 3))

        def attention_pe(pe):
            pe.sem_inc(sem("pv"), PV0)

            def project(p, between=None, ahead=None):
                pe.wait_ge(sem("wq_lo"), p + 2)
                if not isinstance(p, int):
                    pe.wait_ge(sem("m_set"), 4 * p)
                for m in range(2):
                    for c, (at, n) in enumerate(CHUNKS):
                        if m:
                            pe.wait_ge(sem("raw_set"), 6 * p + c + 1)
                            if c == 2 and ahead:
                                ahead()
                        for k in range(KD):
                            last = three(pe, bank(c, 128, n), wqhi[:, m, k, :], wqlo[:, m, k, :],
                                         xthi[:, k, at:at + n], xtlo[:, k, at:at + n], k == 0, k == KD - 1)
                        last.then_inc(sem("qk_raw"), 1)
                        if m == c == 0 and between:
                            between()

            def rough(p, e, t):
                if t == 0:
                    pe.wait_ge(sem("q_lo"), 2 * p + e + 1)
                    pe.wait_ge(sem("kst_set"), 2 * p + e + 1)
                    pe.wait_ge(sem("raw_set"), 6 * p + 6)
                    if e == 1:
                        pe.wait_ge(sem("m_set"), 4 * p + 2)
                else:
                    pe.wait_ge(sem("max"), 20 * p + 10 * e + t)
                for c, (a, b) in enumerate(((0, 512), (512, 1024), (1024, N))):
                    last = pe.matmul(bank(c, P, b - a), qst[:, e, t * P:(t + 1) * P],
                                     kst[:, e, a:b], start=True, stop=True)
                last.then_inc(sem("rough"), 1)

            def maxima(p, e):
                pe.wait_ge(sem("max"), 20 * p + 10 * e + T)
                for t in range(T):
                    at = (t // 4) * BANK + t % 4 * P
                    last = pe.transpose(ps[0:1, at:at + P], mcol[:, e, t:t + 1], ident[0:P, 0:P])
                last.then_inc(sem("m_raw"), 1)

            def scores(p, e, j):
                g, kp = j // 5, j % 5
                b, ago = place(e, j)
                pe.wait_ge(sem("exp"), PAIR * p + (UNITS * e + j - ago + 1 + 3))
                for z in range(2):
                    kt = 2 * kp + z
                    o = ps[0:P, (3 + b) * BANK + z * GQ:(3 + b) * BANK + (z + 1) * GQ]
                    pe.matmul(o, kst[:, e, kt * P:(kt + 1) * P], qst[:, e, g * GQ:(g + 1) * GQ],
                              start=True, stop=False)
                    last = pe.matmul(o, k2[:, e, kt * P:(kt + 1) * P], q2[:, e, g * GQ:(g + 1) * GQ],
                                     start=False, stop=True)
                last.then_inc(sem("st"), 1)

            def weighted(p, e, j):
                g, kp = j // 5, j % 5
                r = (UNITS * e + j) % RING
                wait_lo(pe, p, e, j)
                if kp == 0:
                    pe.wait_ge(sem("o_row"), 2 * NG * p + (NG * e + g + 1))
                if j == 0:
                    pe.wait_ge(sem("v_set"), 2 * p + e + 1)
                b = (6 + (NG * e + g) % 2) * BANK
                for z in range(2):
                    kt = 2 * kp + z
                    hi, lo = prhi[:, r, z * GQ:(z + 1) * GQ], prlo[:, r, z * GQ:(z + 1) * GQ]
                    pe.matmul(ps[:, b:b + GQ], vhi[:, e, kt, :], hi, start=kt == 0, stop=False)
                    pe.matmul(ps[0:HD, b:b + GQ], vlo[:, e, kt, :], hi, start=False, stop=False)
                    last = pe.matmul(ps[:, b:b + GQ], vhi[:, e, kt, :], lo, start=False, stop=kt == T - 1)
                last.then_inc(sem("pv"), 1)

            def start(p, e, between=lambda j: None):
                pe.wait_ge(sem("m_set"), 4 * p + (2 * e + 2))
                pe.wait_ge(sem("qk_split"), 2 * p + (e + 1))
                pe.wait_ge(sem("q2_set"), 2 * p + (e + 1))
                for j in range(LAG):
                    scores(p, e, j)
                    between(j)

            def head(p, e, other):
                for j in range(LAG, UNITS):
                    scores(p, e, j)
                    weighted(p, e, j - LAG)
                    if other is not None and j in ROUGH_AT[e]:
                        rough(*other, ROUGH_AT[e].index(j))
                    if other is not None and j == MAXIMA_AT[e]:
                        maxima(*other)

            def tail(p, e):
                for j in range(UNITS - LAG, UNITS):
                    weighted(p, e, j)

            def pair(p, last):
                head(p, 0, (p, 1))
                if not last:
                    project(p + 1, lambda: tail(p, 0), lambda: start(p, 1))
                    head(p, 1, (p + 1, 0))
                    start(p + 1, 0, lambda j: weighted(p, 1, UNITS - LAG + j))
                else:
                    start(p, 1, lambda j: weighted(p, 0, UNITS - LAG + j))
                    head(p, 1, None)
                    tail(p, 1)

            project(0)
            for t in range(T):
                rough(0, 0, t)
            maxima(0, 0)
            start(0, 0)
            with pe.Fori(0, H // 2 - 1) as p:
                pair(p, False)
            pair(H // 2 - 1, True)

        def attention_act(act):
            def split_qk(p):
                act.wait_ge(sem("wq_in"), 32 * p + 32)
                if not isinstance(p, int):
                    act.wait_ge(sem("qk_raw"), 6 * p)
                act.activation(wqhi[:, :, :, :].rearrange("p m k c -> p (m k c)"),
                               wqst[:, :, :, :].rearrange("p m k c -> p (m k c)"), ACT.Copy).then_inc(sem("wq_hi"), 1)

            def set_raw(p, chunks=range(6)):
                if not isinstance(p, int) and chunks[0] == 0:
                    act.wait_ge(sem("qk_split"), 2 * p)
                for j in chunks:
                    m, c = j // 3, j % 3
                    at, n = CHUNKS[c]
                    act.wait_ge(sem("qk_raw"), 6 * p + (j + 1))
                    act.activation(raw[:, m, at:at + n], bank(c, 128, n), ACT.Copy).then_inc(sem("raw_set"), 1)

            def set_k(p, e):
                r = 64 * e
                act.wait_ge(sem("raw_set"), 6 * p + 6)
                act.wait_ge(sem("q_hi"), 2 * p + e + 1)
                act.activation(kst[64 - r:128 - r, e, :], raw[r:r + 64, 1, :], ACT.Copy).then_inc(sem("kst_set"), 1)

            def set_q(p, e):
                r = 64 * e
                act.activation(q2[r:r + 64, e, :], qst[r:r + 64, e, :].bitcast(f32), ACT.Copy).then_inc(sem("q2_set"), 1)

            def set_m(p, e):
                r = 64 * (1 - e)
                act.wait_ge(sem("m_raw"), 2 * p + e + 1)
                act.activation(halves(q2[r:r + 1, e, 0:1000]), two(0, 1, 500), ACT.Copy).then_inc(sem("m_set"), 1)
                act.activation(q2[r:r + 1, e, 1000:N], bank(2, 1, 250), ACT.Copy).then_inc(sem("m_set"), 1)

            def exps(p, e, between):
                for j in range(UNITS):
                    n = UNITS * e + j
                    act.wait_ge(sem("st"), PAIR * p + (n + 1))
                    act.wait_ge(sem("pv"), PAIR * p + (n + 1 + PV0 - RING))
                    act.activation(prhi[:, n % RING, :], bank(3 + n % 3, P, 2 * GQ), ACT.Exp, scale=float(HD) ** -0.5)
                    wait_lo(act, p, e, j - place(e, j)[1])
                    act.activation(prob[:, n % 3, :], bank(3 + n % 3, P, 2 * GQ), ACT.Exp, scale=float(HD) ** -0.5)\
                        .then_inc(sem("exp"), 1)
                    if j in between:
                        between[j]()

            def pair(p, last):
                steps = {SET_K_AT: lambda: set_k(p, 1), SET_Q_AT: lambda: set_q(p, 1), SET_M_AT[0]: lambda: set_m(p, 1)}
                more = {}
                if not last:
                    steps[SPLIT_QK_AT] = lambda: split_qk(p + 1)
                    more = {LAG - 1: lambda: set_raw(p + 1, (5,)), SET_K_AT: lambda: set_k(p + 1, 0),
                            SET_Q_AT: lambda: set_q(p + 1, 0), SET_M_AT[1]: lambda: set_m(p + 1, 0)}
                else:
                    for k in range(KD):
                        (steps, more)[k // 3][5 * (k % 3) + 9] = lambda k=k: split_act(act, 3, wpst, wphi, (k,))
                exps(p, 0, steps)
                if not last:
                    set_raw(p + 1, range(5))
                exps(p, 1, more)

            act.sem_inc(sem("exp"), 3)
            split_qk(0)
            set_raw(0)
            set_k(0, 0)
            set_q(0, 0)
            set_m(0, 0)
            with act.Fori(0, H // 2 - 1) as p:
                pair(p, False)
            pair(H // 2 - 1, True)

        def lower(eng, p, e, j, done):
            n = UNITS * e + j
            eng.wait_ge(sem("exp"), PAIR * p + (n + 1 + 3))
            if done == "pr_lo_pool":
                alone(eng)
            eng.tensor_tensor(prlo[:, n % RING, :], prob[:, n % 3, :], prhi[:, n % RING, :].bitcast(f32), ALU.subtract)\
                .then_inc(sem(done), 1)

        def attention_dve(dve, order):
            dve.sem_inc(sem("o_row"), 2)
            dve.sem_inc(sem("pr_lo"), 3)
            dve.wait_ge(sem("heads_clear"), 1)

            def split(p, e, step):
                r = 64 * e
                if step == 0:
                    dve.wait_ge(sem("raw_set"), 6 * p + 6)
                    if not isinstance(p, int) or p > 0:
                        dve.wait_ge(sem("st"), PAIR * p + (UNITS * e - UNITS))
                    dve.tensor_copy(qst[r:r + 64, e, :], raw[r:r + 64, 0, :]).then_inc(sem("q_hi"), 1)
                elif step == 1:
                    dve.tensor_copy(kst[r:r + 64, e, :], raw[r:r + 64, 1, :]).then_inc(sem("k_hi"), 1)
                elif step == 2:
                    dve.wait_ge(sem("q_hi"), 2 * p + e + 1)
                    dve.tensor_tensor(qst[64 - r:128 - r, e, :], raw[r:r + 64, 0, :], qst[r:r + 64, e, :].bitcast(f32),
                                      ALU.subtract).then_inc(sem("q_lo"), 1)
                else:
                    dve.wait_ge(sem("k_hi"), 2 * p + e + 1)
                    dve.tensor_tensor(k2[r:r + 64, e, :], raw[r:r + 64, 1, :], kst[r:r + 64, e, :].bitcast(f32),
                                      ALU.subtract).then_inc(sem("qk_split"), 1)

            def maximum(p, e, t):
                dve.wait_ge(sem("rough"), 20 * p + (10 * e + t + 1))
                dve.tensor_reduce(mcol[:, e, t:t + 1], ps[0:P, 0:N], AX.X, ALU.max, negate=True).then_inc(sem("max"), 1)

            def outputs(p, e, g):
                slot = (NG * e + g) % 2
                dve.wait_ge(sem("pv"), PAIR * p + (UNITS * e + 5 * g + 5 + PV0))
                if e == g == 0:
                    dve.wait_ge(sem("v_set"), 2 * p + 2)
                b = (6 + slot) * BANK
                order.did(dve.reciprocal(rz[:, slot, :], ps[HD:2 * HD, b:b + GQ]))
                order.wait()
                dve.tensor_tensor(outt[64 * e:64 * e + HD, ds(p, 1), g * GQ:(g + 1) * GQ].rearrange("c o q -> c (o q)"),
                                  ps[0:HD, b:b + GQ], rz[:, slot, :], ALU.mult).then_inc(sem("o_row"), 1)

            def head(p, e, other):
                for j in range(UNITS):
                    if other is not None and j in ROUGH_AT[e]:
                        maximum(*other, ROUGH_AT[e].index(j))
                    if not by_pool(j):
                        lower(dve, p, e, j, "pr_lo")
                    if j in OUT_AT[e]:
                        outputs(p, e, OUT_AT[e].index(j))
                    if other is not None and 0 <= j - SPLIT_AT[e] < 4:
                        split(*other, j - SPLIT_AT[e])
                outputs(p, e, NG - 1)

            def pair(p, last):
                head(p, 0, (p, 1))
                head(p, 1, None if last else (p + 1, 0))

            for step in range(4):
                split(0, 0, step)
            for t in range(T):
                maximum(0, 0, t)
            with dve.Fori(0, H // 2 - 1) as p:
                order.loop(p, 2 * NG)
                pair(p, False)
            order.end(H // 2 - 1)
            pair(H // 2 - 1, True)

        def experts_pe(pe):
            def expert(e):
                pe.wait_ge(sem("w1_lo"), e + 2)
                for c, (at, n) in enumerate(CHUNKS):
                    for f in range(KF):
                        j = KF * c + f
                        pe.wait_ge(sem("gelu"), 9 * e + (j + 1))
                        for k in range(KD):
                            last = three(pe, bank(j % 3, 128, n), w1hi[:, k, f * 128:(f + 1) * 128],
                                         w1lo[:, k, f * 128:(f + 1) * 128], yhi[:, k, at:at + n],
                                         ylo[:, k, at:at + n], k == 0, k == KD - 1)
                        last.then_inc(sem("hid"), 1)
                pe.wait_ge(sem("w2_lo"), e + 2)
                for t in range(T):
                    u = t % 2
                    c = next(c for c, (at, n) in enumerate(CHUNKS) if (t + 1) * P <= at + n)
                    pe.wait_ge(sem("ht"), 9 * e + KF * (c + 1))
                    pe.wait_ge(sem("added"), T * e + (t + 1))
                    for h in range(2):
                        for f in range(KF):
                            last = three(pe, bank(3 + 2 * u + h, P, HALF), hthi[:, f, t * P:(t + 1) * P],
                                         htlo[:, f, t * P:(t + 1) * P], w2hi[:, f, h * HALF:(h + 1) * HALF],
                                         w2lo[:, f, h * HALF:(h + 1) * HALF], f == 0, f == KF - 1)
                    last.then_inc(sem("ey"), 1)
            with pe.Fori(0, NE) as e:
                expert(e)

        block = ctx.enter_context(nc.Block())

        x_t = x.rearrange("(t p) d -> p t d", p=P)
        bcast = lambda v: v.rearrange("(o d) -> o d", o=1).broadcast_to([P, D])
        PH_EDGES, PH_H1, PH_G1, PH_H2, PH_G2, PH_V, PH_ATT, PH_O, PH_T, PH_R = range(1, 11)

        @block.sync
        def _(sp):
            sp.wait_ge(sem("eraw_clear"), 1)
            for a, e in ((0, src), (1, dst)):
                sp.dma_start(eraw[:, a, 0:2, :], e[0:256 * 128].rearrange("(c p k) -> p c k", c=2, p=128)).then_inc(sem("edges_in"), 16)
                full = EDGES // 128 - 256
                sp.dma_start(eraw[0:full, a, 2, :], e[256 * 128:(256 + full) * 128].rearrange("(p k) -> p k", p=full)).then_inc(sem("edges_in"), 16)
                sp.dma_start(eraw[full:full + 1, a, 2, 0:EDGES % 128],
                             e[(256 + full) * 128:EDGES].rearrange("(p k) -> p k", p=1)).then_inc(sem("edges_in"), 16)
            load_split_sp(sp, 0, gw1, wst)
            for g in range(2):
                sp.dma_start(xall[:, 5 * g:5 * g + 5, :], x_t[:, 5 * g:5 * g + 5, :]).then_inc(sem(f"x_in{g}"), 16)
            sp.dma_start(att[:, 0, :], bcast(gas1)).then_inc(sem("att_in"), 16)
            sp.dma_start(att[:, 1, :], bcast(gad1)).then_inc(sem("att_in"), 16)
            sp.dma_start(brow[:, :], bcast(gb1)).then_inc(sem("brow_in"), 16)
            leave(sp, "sync")
            leave(sp, "sync")
            enter(sp, "sync", PH_H1, ("tensor", "vector", "scalar"))
            sp.dma_start(att[:, 0, :], bcast(gas2)).then_inc(sem("att_in"), 16)
            sp.dma_start(att[:, 1, :], bcast(gad2)).then_inc(sem("att_in"), 16)
            load_split_sp(sp, 1, gw2, wst)
            sp.sem_inc(sem("g1_out0"), 16)
            sp.sem_inc(sem("g1_out1"), 16)
            with sp.Fori(0, T // 2) as i:
                for u in range(2):
                    sp.wait_ge(sem("g1_row"), 2 * i + u + 1)
                    sp.dma_start(hid_d.rearrange("(t p) d -> p t d", p=P)[:, ds(2 * i + u, 1), :], tin[:, u, :])\
                        .then_inc(sem(f"g1_out{u}"), 16)
            for u in range(2):
                sp.wait_ge(sem(f"g1_out{u}"), 16 * (T // 2 + 1))
            sp.dma_start(brow[:, :], bcast(gb2)).then_inc(sem("brow_in"), 16)
            leave(sp, "sync")
            ring_sp(sp, 1, hid_d, tin)
            leave(sp, "sync")
            enter(sp, "sync", PH_H2)
            sp.dma_start(lnrow[:, 0, :], bcast(ln1g)).then_inc(sem("lnrow_in"), 16)
            sp.dma_start(lnrow[:, 1, :], bcast(ln1b)).then_inc(sem("lnrow_in"), 16)
            for u in range(2):
                for n in ("x1", "xa", "xn"):
                    sp.sem_inc(sem(f"{n}_out{u}"), 16)
                sp.dma_start(xres[:, u, :], x_t[:, u, :]).then_inc(sem(f"xres_in{u}"), 16)
            def g2_rows(t, u, more):
                if more:
                    sp.wait_ge(sem("xres_free"), t + 1)
                    sp.dma_start(xres[:, u, :], x_t[:, ds(t + 2, 1), :]).then_inc(sem(f"xres_in{u}"), 16)
                for n, dram, buf in (("x1", x1_d, tin), ("xa", xa_d, xab), ("xn", xn_d, xnb)):
                    sp.wait_ge(sem(f"{n}_row"), t + 1)
                    sp.dma_start(dram.rearrange("(t p) d -> p t d", p=P)[:, ds(t, 1), :], buf[:, u, :])\
                        .then_inc(sem(f"{n}_out{u}"), 16)
            with sp.Fori(0, T // 2 - 1) as i:
                for u in range(2):
                    g2_rows(2 * i + u, u, True)
            sp.wait_ge(sem("left_tensor"), PH_G2)
            for k in range(KD):
                sp.dma_start(wvst[:, k, :], wqkv[k * 128:(k + 1) * 128, 2 * D:3 * D]).then_inc(sem(f"w_in{k % 2}"), 16)
            for u in range(2):
                sp.wait_ge(sem(f"xn_out{u}"), 16 * 2)
                sp.dma_start(vtin[:, u, :], xn_d.rearrange("(t p) d -> p t d", p=P)[:, u, :]).then_inc(sem(f"tile_in{u}"), 16)
            for u in range(2):
                g2_rows(T - 2 + u, u, False)
            for u in range(2):
                for n in ("x1", "xa", "xn"):
                    sp.wait_ge(sem(f"{n}_out{u}"), 16 * (T // 2 + 1))
            leave(sp, "sync")
            enter(sp, "sync", PH_G2)
            ring_sp(sp, 2, xn_d, vtin, start=1)
            leave(sp, "sync")
            enter(sp, "sync", PH_V)
            def load_qk(p):
                sp.wait_ge(sem("wq_lo"), p + 1)
                for m in range(2):
                    sp.dma_start(wqst[:, m, :, :], wqkv.rearrange("(k r) c -> r k c", r=128)[:, :, ds(m * D + p * 128, 128)])\
                        .then_inc(sem("wq_in"), 16)

            load_qk(0)
            with sp.Fori(0, H // 2 - 1) as p:
                load_qk(p + 1)
            sp.wait_ge(sem("qk_raw"), 6 * (H // 2))
            load_split_sp(sp, 3, wproj, wpst)
            leave(sp, "sync")
            enter(sp, "sync", PH_ATT)
            sp.dma_start(row2[:, 0, :], bcast(ln2g)).then_inc(sem("row2_in"), 16)
            sp.dma_start(row2[:, 1, :], bcast(ln2b)).then_inc(sem("row2_in"), 16)
            with sp.Fori(0, T // 2) as i:
                for u in range(2):
                    for n, dram, ring in (("xar", xa_d, xain), ("x1r", x1_d, x1in)):
                        sp.wait_ge(sem(f"{n}_free"), 2 * i + u + 1)
                        sp.dma_start(ring[:, u, :], dram.rearrange("(t p) d -> p t d", p=P)[:, ds(2 * i + u, 1), :])\
                            .then_inc(sem(f"{n}_in{u}"), 16)
            leave(sp, "sync")
            enter(sp, "sync", PH_O)
            leave(sp, "sync")
            def load_w1(e):
                sp.wait_ge(sem("w1_lo"), e + 1)
                sp.dma_start(w1st[:, :, :], w1.rearrange("e (k r) f -> e r k f", r=128)[ds(e, 1), :, :, :]
                             .rearrange("o r k f -> (o r) k f")).then_inc(sem("w1_in"), 16)

            def load_w2(e):
                sp.wait_ge(sem("w2_lo"), e + 1)
                sp.dma_start(w2st[:, :, :], w2.rearrange("e (k r) f -> e r k f", r=128)[ds(e, 1), :, :, :]
                             .rearrange("o r k f -> (o r) k f")).then_inc(sem("w2_in"), 16)
            load_w1(0)
            load_w2(0)
            enter(sp, "sync", PH_T, ("tensor", "vector", "scalar"))
            sp.dma_start(wrst[:, :, :], wrouter.rearrange("(k r) e -> r k e", r=128)).then_inc(sem("wr_in"), 16)
            leave(sp, "sync")
            leave(sp, "sync")
            with sp.Fori(0, NE - 1) as e:
                load_w1(e + 1)
                load_w2(e + 1)
            for t in range(T):
                sp.wait_ge(sem("final"), t + 1)
                sp.dma_start(out.rearrange("(t p) d -> p t d", p=P)[:, t, :], acc[:, t, :]).then_inc(sem("out"), 16)
            sp.wait_ge(sem("out"), 16 * T)

        @block.gpsimd
        def _(pool):
            order = Order(pool, sem("pool_order"))
            pool.memset(eraw[:, :, :, :], -1).then_inc(sem("eraw_clear"), 1)
            order.did(pool.memset(ident[:, :], 0.0))
            order.did(pool.memset(ones[:, :], 1.0))
            order.did(pool.memset(edge[:, :, :], -1.0))
            order.did(pool.iota(iota[:, :], [[1, N]], base=0, channel_multiplier=0, allow_small_or_imprecise_dtypes=True))
            order.did(pool.iota(selfc[:, :], [[P, T]], base=0, channel_multiplier=1, allow_small_or_imprecise_dtypes=True))
            for j in range(T):
                start = 0 if j == 0 else STRIDE * (j - 1) + WINDOW
                end = STRIDE * j + WINDOW if j < T - 1 else ECOLS
                if start < end:
                    order.did(pool.memset(lohi[:, 0, start:end], float(P * j)))
                start, end = STRIDE * j, (STRIDE * (j + 1) if j < T - 1 else ECOLS)
                order.did(pool.memset(lohi[:, 1, start:end], float(P * (j + 1))))
            order.wait()
            order.did(pool.affine_select(out=ident[:, :], in_=ident[:, :], compare_op=ALU.not_equal, fill=1.0,
                                         base=0, pattern=[[-1, 128]], channel_multiplier=1))
            order.wait()
            pool.sem_inc(sem("consts"), 1)
            split_pool(pool, 0, wst, whi, wlo)
            leave(pool, "gpsimd")
            leave(pool, "gpsimd")
            enter(pool, "gpsimd", PH_H1, ("tensor", "vector", "scalar"))
            agg_pool(pool, 0, early=lambda k: split_pool(pool, 1, wst, whi, wlo, (2 * k, 2 * k + 1)))
            leave(pool, "gpsimd")
            leave(pool, "gpsimd")
            enter(pool, "gpsimd", PH_H2)

            def affine(t, u):
                pool.wait_ge(sem("xn_normed"), t + 1)
                pool.tensor_tensor(xnb[:, u, :], xnb[:, u, :], lnrow[:, 0, :], ALU.mult).then_inc(sem("xn_scaled"), 1)
                pool.wait_ge(sem("xn_scaled"), t + 1)
                pool.tensor_tensor(xnb[:, u, :], xnb[:, u, :], lnrow[:, 1, :], ALU.add).then_inc(sem("xn_row"), 1)
            pool.wait_ge(sem("lnrow_in"), 32)
            agg_pool(pool, 1, affine)
            leave(pool, "gpsimd")
            enter(pool, "gpsimd", PH_G2)
            pool.sem_inc(sem("v_copied"), 2)

            def whole(t, u):
                for part, tile, big in (("hi", vxhi, xthi), ("lo", vxlo, xtlo)):
                    if part == "hi":
                        pool.wait_ge(sem("tile_hi"), t + (2 * T + 1))
                    else:
                        pool.wait_ge(sem("tile_lo"), t + (2 * T + 3))
                    alone(pool)
                    last = pool.tensor_copy(big[:, :, ds(t * P, P)], tile[:, u, :].rearrange("p (k c) -> p k c", k=KD))
                last.then_inc(sem("v_copied"), 1)
            with pool.Fori(0, T // 2) as i:
                whole(2 * i, 0)
                whole(2 * i + 1, 1)
            leave(pool, "gpsimd")
            enter(pool, "gpsimd", PH_V)
            pool.sem_inc(sem("wq_lo"), 1)

            def split_qk(p):
                pool.wait_ge(sem("wq_hi"), p + 1)
                pool.tensor_tensor(wqlo[:, :, :, :], wqst[:, :, :, :], wqhi[:, :, :, :].bitcast(f32), ALU.subtract)\
                    .then_inc(sem("wq_lo"), 1)


            def set_v(p, e, part):
                values = val[:, ds(p, 1), :, HD * e:HD * (e + 1)].rearrange("p o t c -> p (o t) c")
                if part == 0:
                    pool.wait_ge(sem("pv"), PAIR * p + (UNITS * e - UNITS + PV0))
                    alone(pool)
                    pool.tensor_copy(vhi[:, e, :, 0:HD], values).then_inc(sem("v_hi"), 1)
                else:
                    pool.wait_ge(sem("v_hi"), 2 * p + (e + 1))
                    alone(pool)
                    pool.tensor_tensor(vlo[:, e, :, :], values, vhi[:, e, :, 0:HD].bitcast(f32), ALU.subtract)\
                        .then_inc(sem("v_set"), 1)

            def head(p, e, steps):
                for j in range(UNITS):
                    if by_pool(j):
                        lower(pool, p, e, j, "pr_lo_pool")
                    if j in steps:
                        steps[j]()

            pool.sem_inc(sem("pr_lo_pool"), 3)
            split_qk(0)
            order.did(pool.memset(q2[:, :, :].bitcast(f32), 0.0))
            order.did(pool.memset(k2[:, :, :].bitcast(f32), 0.0))
            order.did(pool.memset(vhi[:, :, :, HD:].bitcast(f32), 1.0))
            order.wait()
            order.did(pool.memset(k2[64:65, 0, :].bitcast(f32), 1.0))
            order.did(pool.memset(k2[0:1, 1, :].bitcast(f32), 1.0))
            order.wait()
            pool.sem_inc(sem("heads_clear"), 1)
            set_v(0, 0, 0)
            set_v(0, 0, 1)
            with pool.Fori(0, H // 2 - 1) as p:
                head(p, 0, {0: lambda: set_v(p, 1, 0), 5: lambda: set_v(p, 1, 1), 10: lambda: split_qk(p + 1)})
                head(p, 1, {0: lambda: set_v(p + 1, 0, 0), 5: lambda: set_v(p + 1, 0, 1)})
            steps, more = {0: lambda: set_v(H // 2 - 1, 1, 0), 5: lambda: set_v(H // 2 - 1, 1, 1)}, {}
            for k in range(KD):
                (steps, more)[k // 3][5 * (k % 3) + 10] = lambda k=k: split_pool(pool, 3, wpst, wphi, wplo, (k,))
            head(H // 2 - 1, 0, steps)
            head(H // 2 - 1, 1, more)
            leave(pool, "gpsimd")
            enter(pool, "gpsimd", PH_ATT)
            pool.sem_inc(sem("x1r_free"), 2)
            pool.wait_ge(sem("row2_in"), 32)

            def second(t, u, i):
                xt_ = xn2[:, ds(t, 1), :].rearrange("p o d -> p (o d)")
                at_ = acc[:, ds(t, 1), :].rearrange("p o d -> p (o d)")
                pool.wait_ge(sem("n2_normed"), t + 1)
                alone(pool)
                pool.tensor_tensor(xt_, xt_, row2[:, 0, :], ALU.mult).then_inc(sem("n2_scaled"), 1)
                pool.wait_ge(sem(f"x1r_in{u}"), 16 * i + 16)
                alone(pool)
                pool.tensor_tensor(at_, at_, x1in[:, u, :], ALU.add).then_inc(sem("x1r_free"), 1)
                pool.wait_ge(sem("n2_scaled"), t + 1)
                alone(pool)
                pool.tensor_tensor(xt_, xt_, row2[:, 1, :], ALU.add).then_inc(sem("n2_row"), 1)
            with pool.Fori(0, T // 2) as i:
                second(2 * i, 0, i)
                second(2 * i + 1, 1, i)
            leave(pool, "gpsimd")
            enter(pool, "gpsimd", PH_O)
            pool.sem_inc(sem("w1_lo"), 1)
            pool.sem_inc(sem("w2_lo"), 1)

            def split_w(n, e, st, hi, lo):
                pool.wait_ge(sem(f"{n}_hi"), e + 1)
                pool.tensor_tensor(lo[:, :, :], st[:, :, :], hi[:, :, :].bitcast(f32), ALU.subtract)\
                    .then_inc(sem(f"{n}_lo"), 1)
            split_w("w1", 0, w1st, w1hi, w1lo)
            leave(pool, "gpsimd")
            enter(pool, "gpsimd", PH_T, ("tensor", "vector", "scalar"))
            pool.iota(iota8[:, :], [[1, NE]], base=0, channel_multiplier=0, allow_small_or_imprecise_dtypes=True)\
                .then_inc(sem("iota8"), 1)
            leave(pool, "gpsimd")
            with pool.Fori(0, NE - 1) as e:
                split_w("w2", e, w2st, w2hi, w2lo)
                split_w("w1", e + 1, w1st, w1hi, w1lo)
            split_w("w2", NE - 1, w2st, w2hi, w2lo)

        @block.tensor
        def _(pe):
            pe.wait_ge(sem("consts"), 1)
            pe.wait_ge(sem("edges_f"), 1)
            for a in range(2):
                for c in range(3):
                    last = pe.transpose(ps[:, a * BANK + c * 128:a * BANK + (c + 1) * 128], efl[:, a, c, :], ident[:, :])
            last.then_inc(sem("edges_t"), 1)
            pe.wait_ge(sem("viol"), 1)
            pe.matmul(ps[0:1, 2 * BANK:2 * BANK + 1], viol[:, 0:1], viol[:, 1:2], start=True, stop=True).then_inc(sem("viol_sum"), 1)
            pe.wait_ge(sem("flag"), 1)
            spread = pe.value_load(flag[0:1, 0:1], min_val=0, max_val=1)
            pe.sem_inc(sem("oh_free"), 8)
            pe.sem_inc(sem("block_read"), 2)
            pe.sem_inc(sem("tile_raw"), 2)
            pe.sem_inc(sem("tile_y"), 2)
            pe.sem_inc(sem("agg_raw"), 2)
            pe.sem_inc(sem("agg_sum"), 2)

            def count_edges(steps):
                turns = steps // 8
                with pe.Fori(0, T // 2) as jj:
                    for v in range(2):
                        pe.wait_ge(sem("block_read"), 2 * jj + v + 1)

                        def turn(r, first, last):
                            for u in range(8):
                                pe.wait_ge(sem("oh_ready"), (2 * jj + v) * steps + r * 8 + (u + 1))
                                for c, (a, b) in enumerate(((0, 512), (512, 1024), (1024, N))):
                                    mm = pe.matmul(ps[0:P, (3 * v + c) * BANK:(3 * v + c) * BANK + b - a],
                                                   ohd[:, u % 4, :], ohs[:, u % 4, a:b],
                                                   start=first and u == 0, stop=last and u == 7)
                                mm.then_inc(sem("oh_free"), 1)
                        turn(0, True, False)
                        with pe.Fori(1, turns - 1) as r:
                            turn(r, False, False)
                        turn(turns - 1, False, True)
                        pe.wait_ge(sem("oh_free"), (2 * jj + v + 1) * steps + 8)
                        pe.sem_inc(sem("block_done"), 1)
            with pe.If(spread == 0):
                count_edges(NEAR_STEPS)
            with pe.Else():
                count_edges(ALL_STEPS)
            leave(pe, "tensor")
            enter(pe, "tensor", PH_EDGES)

            def ready_x(t, u):
                pe.wait_ge(sem("h1_row"), t + 1)
            pe.wait_ge(sem("w_lo"), KD * 1)
            gemm_pe(pe, 0, lambda t, u: tin[:, u, :], ready_x, txhi, txlo, whi, wlo)
            leave(pe, "tensor")
            enter(pe, "tensor", PH_H1, ("vector", "scalar"))
            agg_pe(pe, 0)
            leave(pe, "tensor")
            enter(pe, "tensor", PH_G1)
            pe.wait_ge(sem("w_lo"), KD * 2)

            def slot_ready(m):
                def ready(t, u):
                    pe.wait_ge(sem(f"tile_in{u}"), 8 * t + (8 * T * m + 16 - 8 * u))
                return ready
            gemm_pe(pe, 1, lambda t, u: tin[:, u, :], slot_ready(0), txhi, txlo, whi, wlo)
            leave(pe, "tensor")
            enter(pe, "tensor", PH_H2, ("vector", "scalar"))
            agg_pe(pe, 1)
            leave(pe, "tensor")
            enter(pe, "tensor", PH_G2, ("vector", "scalar"))
            pe.wait_ge(sem("w_lo"), KD * 3)
            gemm_pe(pe, 2, lambda t, u: vtin[:, u, :], slot_ready(1), vxhi, vxlo, wvhi, wvlo)
            leave(pe, "tensor")
            enter(pe, "tensor", PH_V)
            attention_pe(pe)
            leave(pe, "tensor")
            enter(pe, "tensor", PH_ATT)
            pe.wait_ge(sem("w_lo"), KD * 4)
            gemm_pe(pe, 3, None, None, oxhi, oxlo, wphi, wplo)
            leave(pe, "tensor")
            enter(pe, "tensor", PH_O)
            for t in range(T):
                pe.wait_ge(sem("t2_lo"), t + 1)
                for k in range(KD):
                    at = (t % 4 * 2 + k // 3) * BANK + k % 3 * P
                    last = pe.transpose(ps[:, at:at + P], xn2[:, t, k * 128:(k + 1) * 128], ident[0:P, 0:P])
                last.then_inc(sem("t2_raw"), 1)
            leave(pe, "tensor")
            enter(pe, "tensor", PH_T)
            pe.wait_ge(sem("wr_split"), 1)
            for c, (at, n) in enumerate(CHUNKS):
                for k in range(KD):
                    last = three(pe, bank(c, NE, n), wrhi[:, k, :], wrlo[:, k, :], yhi[:, k, at:at + n],
                                 ylo[:, k, at:at + n], k == 0, k == KD - 1)
                last.then_inc(sem("logt_raw"), 1)
            pe.wait_ge(sem("logt"), 3)
            for t in range(T):
                last = pe.transpose(ps[0:P, 3 * BANK + t * NE:3 * BANK + (t + 1) * NE], logt[:, t * P:(t + 1) * P], ident[0:NE, 0:NE])
            last.then_inc(sem("logit_raw"), 1)
            leave(pe, "tensor")
            enter(pe, "tensor", PH_R, ("vector", "scalar"))
            experts_pe(pe)

        @block.scalar
        def _(act):
            split_act(act, 0, wst, whi)
            for t in range(T):
                act.wait_ge(sem(f"x_in{t // 5}"), 16)
                if t:
                    act.wait_ge(sem("ln_sum"), t)
                act.activation(esb[:, 0:D], xall[:, t, :], ACT.Copy, accum_out=lnc[:, t, 0:1]).then_inc(sem("ln_sum"), 1)
            act.wait_ge(sem("ln_sum"), T)
            act.activation(lnc[:, :, 1:2], lnc[:, :, 0:1], ACT.Copy, scale=-1.0 / D).then_inc(sem("ln_mean"), 1)
            act.wait_ge(sem("ln_mean"), 1)
            for t in range(T):
                act.activation(xall[:, t, :], xall[:, t, :], ACT.Identity, bias=lnc[:, t, 1:2]).then_inc(sem("ln_cen"), 1)
            act.wait_ge(sem("ln_cen"), T)
            for t in range(T):
                if t:
                    act.wait_ge(sem("ln_sq"), t)
                act.activation(esb[:, 0:D], xall[:, t, :], ACT.Square, accum_out=lnc[:, t, 2:3]).then_inc(sem("ln_sq"), 1)
            act.wait_ge(sem("ln_sq"), T)
            act.wait_ge(sem("eps"), 1)
            act.activation(lnc[:, :, 4:5], lnc[:, :, 2:3], ACT.Sqrt, scale=1.0 / D, bias=viol[0:P, 3:4])\
                .then_inc(sem("ln_sqrt"), 1)
            with act.Fori(0, T // 2) as jj:
                for v in range(2):
                    act.wait_ge(sem("block_done"), 2 * jj + v + 1)
                    got = ps[0:P, 3 * v * BANK:3 * v * BANK + N]
                    act.activation(cnt[:, ds(2 * jj + v, 1), :].rearrange("p o n -> p (o n)"), got, ACT.Copy)
                    act.activation(far[:, ds(2 * jj + v, 1), :].rearrange("p o n -> p (o n)"), got, ACT.Relu,
                                   scale=-FAR, bias=viol[0:P, 2:3]).then_inc(sem("block_read"), 1)
            act.wait_ge(sem("ln_rstd"), 1)
            leave(act, "scalar")
            enter(act, "scalar", PH_EDGES, ("vector",))

            def normed(t, u):
                act.wait_ge(sem("tile_raw"), t + 1)
                act.activation(tin[:, u, :], xall[:, ds(t, 1), :].rearrange("p o d -> p (o d)"), ACT.Copy,
                               scale=lnc[:, ds(t, 1), 5:6].rearrange("p o c -> p (o c)")).then_inc(sem("h1_row"), 1)
            h_phase_act(act, 0, normed)
            leave(act, "scalar")
            enter(act, "scalar", PH_H1, ("tensor", "vector"))
            agg_act(act, 0, lambda s, k: split_act(act, 1, wst, whi, (2 * k, 2 * k + 1)) if k < 3 else None)
            leave(act, "scalar")
            enter(act, "scalar", PH_G1)
            h_phase_act(act, 1)
            leave(act, "scalar")
            enter(act, "scalar", PH_H2)

            def norms(s, k):
                a, b = 0 <= k - 2 < T, 0 <= k - 3 < T
                u, v = k % 2, (k - 3) % 2
                if a:
                    act.wait_ge(sem("var_a"), s - 1)
                    act.activation(stat[:, u, 1:2], stat[:, u, 1:2], ACT.Sqrt).then_inc(sem("root_a"), 1)
                if b:
                    act.wait_ge(sem("var_b"), s - 2)
                    act.activation(stat[:, v, 5:6], stat[:, v, 5:6], ACT.Sqrt).then_inc(sem("root_b"), 1)
                if a:
                    act.wait_ge(sem("rstd_a"), s - 1)
                    act.wait_ge(sem(f"xa_out{u}"), 8 * s + (16 - 8 * u) - 16)
                    act.activation(xab[:, u, :], tin[:, u, :], ACT.Identity, scale=stat[:, u, 2:3], bias=stat[:, u, 3:4])\
                        .then_inc(sem("xa_row"), 1)
                if b:
                    act.wait_ge(sem("rstd_b"), s - 2)
                    act.wait_ge(sem(f"xn_out{v}"), 8 * s + (16 - 8 * v) - 24)
                    act.activation(xnb[:, v, :], xab[:, v, :], ACT.Identity, scale=stat[:, v, 6:7], bias=stat[:, v, 7:8])\
                        .then_inc(sem("xn_normed"), 1)
            agg_act(act, 1, norms)
            leave(act, "scalar")
            enter(act, "scalar", PH_G2, ("vector", "tensor"))
            for m in range(2):
                act.wait_ge(sem(f"w_in{m}"), 16 * (KD // 2 * 3))
            for k in range(KD):
                act.activation(wvhi[:, k, :], wvst[:, k, :], ACT.Copy).then_inc(sem("w_hi"), 1)

            def v_hi(t, u):
                act.wait_ge(sem("v_copied"), t + 1)
                gemm_hi(act, 2, vxhi, t, u)

            def v_out(t, u):
                act.wait_ge(sem("tile_y"), t + (2 * T + 3))
                act.activation(val[:, :, ds(t, 1), :].rearrange("p (a r) o c -> p a r (o c)", a=2),
                               two(4 + 2 * u, P, HALF).rearrange("p a (r c) -> p a r c", c=128), ACT.Copy)\
                    .then_inc(sem("tile_yfree"), 1)
            v_hi(0, 0)
            with act.Fori(0, T // 2 - 1) as i:
                v_hi(2 * i + 1, 1)
                v_out(2 * i, 0)
                v_hi(2 * i + 2, 0)
                v_out(2 * i + 1, 1)
            v_hi(T - 1, 1)
            v_out(T - 2, 0)
            v_out(T - 1, 1)
            leave(act, "scalar")
            enter(act, "scalar", PH_V)
            attention_act(act)
            leave(act, "scalar")
            enter(act, "scalar", PH_ATT)

            def norm2(t, u):
                act.wait_ge(sem("var_c"), t + 1)
                act.activation(stat[:, u, 1:2], stat[:, u, 1:2], ACT.Sqrt).then_inc(sem("root_c"), 1)
                act.wait_ge(sem("rstd_c"), t + 1)
                act.activation(xn2[:, ds(t, 1), :].rearrange("p o d -> p (o d)"),
                               acc[:, ds(t, 1), :].rearrange("p o d -> p (o d)"), ACT.Identity,
                               scale=stat[:, u, 2:3], bias=stat[:, u, 3:4]).then_inc(sem("n2_normed"), 1)

            def o_hi(t, u):
                act.wait_ge(sem("tile_y"), t + (3 * T + 1))
                act.activation(oxhi[:, u, :].rearrange("p (k c) -> p k c", k=KD), outt[:, :, ds(t * P, P)], ACT.Copy)\
                    .then_inc(sem("tile_hi"), 1)
            o_hi(0, 0)
            with act.Fori(0, T // 2 - 1) as i:
                o_hi(2 * i + 1, 1)
                norm2(2 * i, 0)
                o_hi(2 * i + 2, 0)
                norm2(2 * i + 1, 1)
            o_hi(T - 1, 1)
            norm2(T - 2, 0)
            norm2(T - 1, 1)
            leave(act, "scalar")
            enter(act, "scalar", PH_O)
            for t in range(T):
                act.wait_ge(sem("t2_raw"), t + 1)
                act.activation(yhi[:, :, t * P:(t + 1) * P].rearrange("p (a k) c -> p a k c", a=2),
                               two(t % 4 * 2, 128, 3 * P).rearrange("p a (k c) -> p a k c", c=P), ACT.Copy)\
                    .then_inc(sem("t2_hi"), 1)
            def split_w(n, e, st, hi):
                act.wait_ge(sem(f"{n}_in"), 16 * e + 16)
                act.activation(hi[:, :, :].rearrange("p k c -> p (k c)"), st[:, :, :].rearrange("p k c -> p (k c)"), ACT.Copy)\
                    .then_inc(sem(f"{n}_hi"), 1)
            split_w("w1", 0, w1st, w1hi)
            leave(act, "scalar")
            enter(act, "scalar", PH_T)
            act.wait_ge(sem("wr_in"), 16)
            act.activation(wrhi[:, :, :], wrst[:, :, :], ACT.Copy).then_inc(sem("wr_hi"), 1)
            for c, (at, n) in enumerate(CHUNKS):
                act.wait_ge(sem("logt_raw"), c + 1)
                act.activation(logt[:, at:at + n], bank(c, NE, n), ACT.Copy).then_inc(sem("logt"), 1)
            act.wait_ge(sem("gap"), 1)
            act.activation(gcol[:, :, 1:2], gcol[:, :, 0:1], ACT.Exp).then_inc(sem("gap_exp"), 1)
            leave(act, "scalar")
            enter(act, "scalar", PH_R, ("vector", "tensor"))
            act.sem_inc(sem("gelu"), 3)

            def expert(e, more):
                act.wait_ge(sem("hid"), 9 * e + 1)
                split_w("w2", e, w2st, w2hi)
                for j in range(KF * len(CHUNKS)):
                    c, f = j // KF, j % KF
                    n = CHUNKS[c][1]
                    act.wait_ge(sem("hid"), 9 * e + (j + 1))
                    act.wait_ge(sem("ht_free"), 9 * e + (j + 1))
                    act.activation(gel[:, j % 3, 0:n], bank(j % 3, 128, n), ACT.Gelu).then_inc(sem("gelu"), 1)
                if more:
                    split_w("w1", e + 1, w1st, w1hi)
            with act.Fori(0, NE - 1) as e:
                expert(e, True)
            expert(NE - 1, False)

        @block.vector
        def _(dve):
            order = Order(dve, sem("dve_order"))
            dve.sem_inc(sem("tile_lo"), 2)
            dve.sem_inc(sem("tile_yfree"), 2)
            dve.sem_inc(sem("agg_lo"), 1)
            dve.sem_inc(sem("agg_read"), 2)
            dve.sem_inc(sem("agg_maxed"), 1)
            dve.wait_ge(sem("consts"), 1)
            dve.wait_ge(sem("edges_in"), 96)
            dve.tensor_copy(efl[:, :, :, :], eraw[:, :, :, :]).then_inc(sem("edges_f"), 1)
            order.did(dve.memset(viol[:, 1:2], 1.0))
            order.did(dve.memset(viol[:, 2:3], FAR))
            dve.memset(viol[:, 3:4], EPS).then_inc(sem("eps"), 1)
            dve.wait_ge(sem("edges_t"), 1)
            order.did(dve.tensor_copy(edge[:, :, LEAD:ECOLS], two(0, 128, 384)))
            order.wait()
            d_ = edge[:, 1, :]
            order.did(dve.tensor_tensor(lohi[:, 0, :], d_, lohi[:, 0, :], ALU.is_lt))
            order.did(dve.tensor_tensor(lohi[:, 1, :], d_, lohi[:, 1, :], ALU.is_ge))
            order.wait()
            order.did(dve.tensor_tensor(lohi[:, 0, :], lohi[:, 0, :], lohi[:, 1, :], ALU.add))
            order.wait()
            dve.scalar_tensor_tensor(lohi[:, 1, :], d_, 0.0, lohi[:, 0, :], ALU.is_ge, ALU.mult, accum_out=viol[:, 0:1])\
                .then_inc(sem("viol"), 1)
            dve.wait_ge(sem("viol_sum"), 1)
            dve.tensor_scalar(flag[0:1, 0:1], ps[0:1, 2 * BANK:2 * BANK + 1], 0.0, None, ALU.is_gt).then_inc(sem("flag"), 1)
            dve.wait_ge(sem("flag"), 1)
            spread = dve.value_load(flag[0:1, 0:1], min_val=0, max_val=1)

            def one_hots(steps, stride):
                turns = steps // 8
                with dve.Fori(0, T) as j:
                    def turn(r, first):
                        for u in range(8):
                            dve.wait_ge(sem("oh_free"), j * steps + r * 8 + (u + 5))
                            if first and u == 0:
                                s_col = d_col = selfc[:, ds(j, 1)]
                            else:
                                q = j * stride + r * 8 + (u - 1)
                                s_col, d_col = edge[:, 0, ds(q, 1)], edge[:, 1, ds(q, 1)]
                            dve.tensor_scalar(ohd[:, u % 4, :], iota[:, ds(j * P, P)], d_col, None, ALU.is_equal)
                            dve.tensor_scalar(ohs[:, u % 4, :], iota[:, :], s_col, None, ALU.is_equal)\
                                .then_inc(sem("oh_ready"), 1)
                    turn(0, True)
                    with dve.Fori(1, turns) as r:
                        turn(r, False)
            with dve.If(spread == 0):
                one_hots(NEAR_STEPS, STRIDE)
            with dve.Else():
                one_hots(ALL_STEPS, 0)
            dve.wait_ge(sem("ln_sqrt"), 1)
            dve.reciprocal(lnc[:, :, 5:6], lnc[:, :, 4:5]).then_inc(sem("ln_rstd"), 1)
            leave(dve, "vector")
            dve.wait_ge(sem("att_in"), 32)
            h_phase_dve(dve, 0)
            diag_dve(dve, 0)
            leave(dve, "vector")
            enter(dve, "vector", PH_H1, ("tensor", "scalar"))
            dve.wait_ge(sem("brow_in"), 16)
            dve.wait_ge(sem("agg_esb"), 2)

            def finish1(t, u):
                dve.wait_ge(sem(f"g1_out{u}"), 8 * t + (16 - 8 * u))
                order.did(dve.scalar_tensor_tensor(halves(tin[:, u, :]), two(3 + 2 * u, P, HALF), zsum[:, u, 5:6],
                                                   halves(brow[:, :]), ALU.mult, ALU.add))
                order.wait()
                dve.sem_inc(sem("agg_read"), 1)
                dve.tensor_scalar(tin[:, u, :], tin[:, u, :], 0.0, None, ALU.max).then_inc(sem("g1_row"), 1)
            nothing = lambda s, k: None
            agg_dve(dve, order, 0, 4, nothing, finish1, nothing)
            leave(dve, "vector")
            enter(dve, "vector", PH_G1, ("scalar", "sync"))
            dve.wait_ge(sem("att_in"), 64)
            h_phase_dve(dve, 1)
            diag_dve(dve, 1)
            leave(dve, "vector")
            enter(dve, "vector", PH_H2, ("tensor", "scalar"))
            dve.wait_ge(sem("brow_in"), 32)
            dve.wait_ge(sem("agg_esb"), 4)

            def moments(row, u, c, v):
                for h in range(2):
                    order.did(dve.bn_stats(bn[:, u, 6 * h:6 * h + 6], row[:, h * HALF:(h + 1) * HALF]))
                order.wait()
                alone(dve)
                order.did(dve.bn_aggr(stat[:, u, c:c + 2], bn[:, u, :]))
                order.wait()
                dve.tensor_scalar(stat[:, u, c + 1:c + 2], stat[:, u, c + 1:c + 2], EPS, None, ALU.add).then_inc(sem(f"var_{v}"), 1)

            def inverse(t, u, c, v):
                dve.wait_ge(sem(f"root_{v}"), t + 1)
                order.did(dve.reciprocal(stat[:, u, c + 2:c + 3], stat[:, u, c + 1:c + 2]))
                order.wait()
                dve.scalar_tensor_tensor(stat[:, u, c + 3:c + 4], stat[:, u, c:c + 1], -1.0, stat[:, u, c + 2:c + 3],
                                         ALU.mult, ALU.mult).then_inc(sem(f"rstd_{v}"), 1)

            def finish2(t, u):
                dve.wait_ge(sem(f"x1_out{u}"), 8 * t + (16 - 8 * u))
                order.did(dve.scalar_tensor_tensor(halves(tin[:, u, :]), two(3 + 2 * u, P, HALF), zsum[:, u, 5:6],
                                                   halves(brow[:, :]), ALU.mult, ALU.add))
                order.wait()
                dve.sem_inc(sem("agg_read"), 1)
                dve.wait_ge(sem(f"xres_in{u}"), 8 * t + (16 - 8 * u))
                order.did(dve.tensor_tensor(tin[:, u, :], tin[:, u, :], xres[:, u, :], ALU.add))
                order.wait()
                dve.sem_inc(sem("xres_free"), 1)
                dve.sem_inc(sem("x1_row"), 1)
                moments(tin[:, u, :], u, 0, "a")

            def before2(s, k):
                if 0 <= k - 3 < T:
                    dve.wait_ge(sem("xa_row"), s - 3 + 1)
                    moments(xab[:, (k - 3) % 2, :], (k - 3) % 2, 4, "b")

            def after2(s, k):
                if 0 <= k - 2 < T:
                    inverse(s - 2, k % 2, 0, "a")
                if 0 <= k - 3 < T:
                    inverse(s - 3, (k - 3) % 2, 4, "b")
            agg_dve(dve, order, 1, 4 + 1 + 2 * 4, before2, finish2, after2)
            leave(dve, "vector")
            enter(dve, "vector", PH_G2, ("tensor", "scalar"))
            for k in range(KD):
                dve.wait_ge(sem("w_hi"), KD * 2 + k + 1)
                dve.tensor_tensor(wvlo[:, k, :], wvst[:, k, :], wvhi[:, k, :].bitcast(f32), ALU.subtract).then_inc(sem("w_lo"), 1)
            with dve.Fori(0, T // 2) as i:
                gemm_lo(dve, 2, vxhi, vxlo, 2 * i, 0)
                gemm_lo(dve, 2, vxhi, vxlo, 2 * i + 1, 1)
            leave(dve, "vector")
            enter(dve, "vector", PH_V)
            attention_dve(dve, order)
            leave(dve, "vector")
            enter(dve, "vector", PH_ATT)
            dve.sem_inc(sem("xar_free"), 2)

            def residual(t, u):
                row = acc[:, ds(t, 1), :].rearrange("p o d -> p (o d)")
                dve.wait_ge(sem("tile_y"), t + (3 * T + 3))
                dve.wait_ge(sem(f"xar_in{u}"), 8 * t + (16 - 8 * u))
                order.did(dve.tensor_tensor(halves(row), two(4 + 2 * u, P, HALF), halves(xain[:, u, :]), ALU.add))
                order.wait()
                dve.sem_inc(sem("xar_free"), 1)
                dve.sem_inc(sem("tile_yfree"), 1)
                moments(row, u, 0, "c")
                inverse(t, u, 0, "c")

            def o_lo(t, u):
                dve.wait_ge(sem("tile_hi"), t + (3 * T + 1))
                dve.tensor_tensor(oxlo[:, u, :].rearrange("p (k c) -> p k c", k=KD), outt[:, :, ds(t * P, P)],
                                  oxhi[:, u, :].rearrange("p (k c) -> p k c", k=KD).bitcast(f32), ALU.subtract)\
                    .then_inc(sem("tile_lo"), 1)
            o_lo(0, 0)
            with dve.Fori(0, T // 2 - 1) as i:
                order.loop(i, 2 * 5)
                o_lo(2 * i + 1, 1)
                residual(2 * i, 0)
                o_lo(2 * i + 2, 0)
                residual(2 * i + 1, 1)
            order.end(T // 2 - 1)
            o_lo(T - 1, 1)
            residual(T - 2, 0)
            residual(T - 1, 1)
            leave(dve, "vector")
            enter(dve, "vector", PH_O)
            dve.sem_inc(sem("t2_lo"), 4)
            for t in range(T):
                dve.wait_ge(sem("t2_hi"), t + 1)
                dve.tensor_tensor(ylo[:, :, t * P:(t + 1) * P].rearrange("p (a k) c -> p a k c", a=2),
                                  two(t % 4 * 2, 128, 3 * P).rearrange("p a (k c) -> p a k c", c=P),
                                  yhi[:, :, t * P:(t + 1) * P].rearrange("p (a k) c -> p a k c", a=2).bitcast(f32),
                                  ALU.subtract).then_inc(sem("t2_lo"), 1)
            leave(dve, "vector")
            enter(dve, "vector", PH_T)
            dve.wait_ge(sem("wr_hi"), 1)
            dve.tensor_tensor(wrlo[:, :, :], wrst[:, :, :], wrhi[:, :, :].bitcast(f32), ALU.subtract).then_inc(sem("wr_split"), 1)
            dve.wait_ge(sem("logit_raw"), 1)
            order.did(dve.tensor_copy(logit[:, :, :].rearrange("p t e -> p (t e)"), ps[0:P, 3 * BANK:3 * BANK + T * NE]))
            order.wait()
            for t in range(T):
                order.did(dve.max(top8[:, t, :], logit[:, t, :]))
            order.wait()
            for t in range(T):
                order.did(dve.max_index(ix8[:, t, :], top8[:, t, :], logit[:, t, :]))
            order.wait()
            order.did(dve.tensor_copy(ixf[:, :, :], ix8[:, :, 0:2]))
            order.did(dve.tensor_tensor(gcol[:, :, 0:1], top8[:, :, 1:2], top8[:, :, 0:1], ALU.subtract))
            order.wait()
            dve.sem_inc(sem("gap"), 1)
            dve.wait_ge(sem("gap_exp"), 1)
            order.did(dve.tensor_scalar(gcol[:, :, 0:1], gcol[:, :, 1:2], 1.0, None, ALU.add))
            order.wait()
            order.did(dve.reciprocal(gcol[:, :, 2:3], gcol[:, :, 0:1]))
            order.wait()
            order.did(dve.tensor_tensor(gcol[:, :, 3:4], gcol[:, :, 1:2], gcol[:, :, 2:3], ALU.mult))
            dve.wait_ge(sem("iota8"), 1)
            for w in range(2):
                order.did(dve.tensor_tensor(hot[:, w, :, :], iota8[:, :].rearrange("p (o e) -> p o e", o=1).broadcast_to([P, T, NE]),
                                            ixf[:, :, w:w + 1].broadcast_to([P, T, NE]), ALU.is_equal))
            order.wait()
            for w in range(2):
                order.did(dve.tensor_tensor(hot[:, w, :, :], hot[:, w, :, :],
                                            gcol[:, :, 2 + w:3 + w].broadcast_to([P, T, NE]), ALU.mult))
            order.wait()
            order.did(dve.tensor_tensor(gate[:, :, :], hot[:, 0, :, :], hot[:, 1, :, :], ALU.add))
            order.wait()
            leave(dve, "vector")
            enter(dve, "vector", PH_R, ("scalar", "tensor"))
            dve.sem_inc(sem("ht_free"), 3)
            dve.sem_inc(sem("added"), 2)

            def expert(e, last):
                for j in range(KF * len(CHUNKS)):
                    c, f = j // KF, j % KF
                    at, n = CHUNKS[c]
                    dve.wait_ge(sem("gelu"), 9 * e + (j + 4))
                    dve.tensor_copy(hthi[:, f, at:at + n], gel[:, j % 3, 0:n]).then_inc(sem("ht_hi"), 1)
                    dve.wait_ge(sem("ht_hi"), 9 * e + (j + 1))
                    dve.tensor_tensor(htlo[:, f, at:at + n], gel[:, j % 3, 0:n], hthi[:, f, at:at + n].bitcast(f32), ALU.subtract)\
                        .then_inc(sem("ht"), 1)
                    dve.wait_ge(sem("ht"), 9 * e + (j + 1))
                    dve.sem_inc(sem("ht_free"), 1)
                for t in range(T):
                    dve.wait_ge(sem("ey"), T * e + (t + 1))
                    dve.scalar_tensor_tensor(halves(acc[:, t, :]), two(3 + 2 * (t % 2), P, HALF), gate[:, t, ds(e, 1)],
                                             halves(acc[:, t, :]), ALU.mult, ALU.add).then_inc(sem("added"), 1)
                    if last:
                        dve.wait_ge(sem("added"), T * e + (t + 3))
                        dve.sem_inc(sem("final"), 1)
            with dve.Fori(0, NE - 1) as e:
                expert(e, False)
            expert(NE - 1, True)


_INS = ['x', 'src', 'dst', 'L0_gnn_W1', 'L0_gnn_att_src1', 'L0_gnn_att_dst1', 'L0_gnn_b1', 'L0_gnn_W2',
        'L0_gnn_att_src2', 'L0_gnn_att_dst2', 'L0_gnn_b2', 'L0_ffn_Wqkv', 'L0_ffn_Wproj', 'L0_ffn_Wrouter',
        'L0_ffn_W1', 'L0_ffn_W2', 'L0_ffn_ln1_g', 'L0_ffn_ln1_b', 'L0_ffn_ln2_g', 'L0_ffn_ln2_b']


def kernel(**inputs):
    import concourse.bacc as _bacc
    from concourse.bass_utils import run_bass_kernel_spmd as _run

    nc = _bacc.Bacc("TRN2", target_bir_lowering=False, num_devices=1)
    arrays, args = {}, []
    for name in _INS:
        a = np.ascontiguousarray(inputs[name])
        arrays[f"in_{name}_dram"] = a
        args.append(nc.dram_tensor(f"in_{name}_dram", a.shape, mybir.dt.from_np(a.dtype), kind="ExternalInput").ap())
    o = nc.dram_tensor("out_0_dram", (N, D), mybir.dt.float32, kind="ExternalOutput").ap()
    build(nc, *args, o)
    r = _run(nc, [arrays], core_ids=[0])
    return r.results[0]["out_0_dram"]
```
